# Optimizing a Trainium2 kernel written in Bass

```python
import numpy as np
import jax
import jax.numpy as jnp

def _softmax(x, axis=-1):
    return jax.nn.softmax(x, axis=axis)

def _gelu(x):
    return jax.nn.gelu(x, approximate=True)

def _silu(x):
    return jax.nn.silu(x)

def _sigmoid(x):
    return jax.nn.sigmoid(x)

def _layernorm(x, axis=-1, eps=1e-05):
    m = jnp.mean(x, axis=axis, keepdims=True)
    v = jnp.var(x, axis=axis, keepdims=True)
    return (x - m) / jnp.sqrt(v + eps)

def _scatter_add(tgt, idx, src, axis=0):
    return tgt.at[idx].add(src)

def _segment_sum(src, seg, n):
    return jax.ops.segment_sum(src, seg, n)
kernel_name = 'mk_seq_postln_d1_jaxref_r4_820253'

def setup_inputs(seed: int=0):
    np.random.seed(seed)
    _w = jnp.asarray

    def _L0_attn_setup():
        import jax, jax.numpy as jnp
        import numpy as np
        _J6 = jnp.array([[0, 0, 0, 0, 0, 1], [0, 0, 0, 0, -1, 0], [0, 0, 0, 1, 0, 0], [0, 0, 1, 0, 0, 0], [0, -1, 0, 0, 0, 0], [1, 0, 0, 0, 0, 0]], dtype=jnp.float32)
        _PAIRS4 = [(0, 1), (0, 2), (0, 3), (1, 2), (1, 3), (2, 3)]

        def exterior(p1, p2):
            parts = [p1[..., i] * p2[..., j] - p1[..., j] * p2[..., i] for i, j in _PAIRS4]
            L = jnp.stack(parts, axis=-1)
            n = jnp.sqrt(jnp.sum(L * L, axis=-1, keepdims=True))
            return L / jnp.maximum(n, 1e-12)
        D, H = (256, 16)
        B, T = (2, 512)
        key = jax.random.key(seed)
        ks = jax.random.split(key, 16)
        s = 0.02
        return {'x': jax.random.normal(ks[0], (B, T, D), dtype=jnp.float32), 'qkv_w': jax.random.normal(ks[1], (D, 3 * D), dtype=jnp.float32) * s, 'qkv_b': jnp.zeros((3 * D,), dtype=jnp.float32), 'w1_write': jax.random.normal(ks[2], (D, 4 * H), dtype=jnp.float32) * s, 'w2_write': jax.random.normal(ks[3], (D, 4 * H), dtype=jnp.float32) * s, 'w1_read': jax.random.normal(ks[4], (D, 4 * H), dtype=jnp.float32) * s, 'w2_read': jax.random.normal(ks[5], (D, 4 * H), dtype=jnp.float32) * s, 'geo_w': jax.random.normal(ks[6], (D, D), dtype=jnp.float32) * s, 'geo_b': jnp.zeros((D,), dtype=jnp.float32), 'gate_w': jax.random.normal(ks[7], (D, H), dtype=jnp.float32) * s, 'gate_b': jnp.zeros((H,), dtype=jnp.float32), 'inc_scale': jnp.ones((H,), dtype=jnp.float32), 'out_w': jax.random.normal(ks[8], (D, D), dtype=jnp.float32) * s, 'out_b': jnp.zeros((D,), dtype=jnp.float32)}
    _L0_attn_in = _L0_attn_setup()

    def _L0_ffn_setup():
        import jax, jax.numpy as jnp
        import numpy as np
        DIM = 256
        HIDDEN = 768
        SCALE = 1.0 / 127.0

        def _dequant(w_int, dtype):
            return w_int.astype(dtype) * jnp.asarray(SCALE, dtype)
        key = jax.random.key(seed)
        k_x, k_g, k_u, k_d = jax.random.split(key, 4)
        x = jax.random.normal(k_x, (4, 512, DIM), dtype=jnp.float32)
        w_gate = jax.random.randint(k_g, (HIDDEN, DIM), -127, 128, dtype=jnp.int32)
        w_up = jax.random.randint(k_u, (HIDDEN, DIM), -127, 128, dtype=jnp.int32)
        w_down = jax.random.randint(k_d, (DIM, HIDDEN), -127, 128, dtype=jnp.int32)
        return {'x': x, 'w_gate': w_gate, 'w_up': w_up, 'w_down': w_down}
    _L0_ffn_in = _L0_ffn_setup()
    _d = {'L0_attn_x': _L0_attn_in['x'], 'L0_attn_qkv_w': _L0_attn_in['qkv_w'], 'L0_attn_qkv_b': _L0_attn_in['qkv_b'], 'L0_attn_w1_write': _L0_attn_in['w1_write'], 'L0_attn_w2_write': _L0_attn_in['w2_write'], 'L0_attn_w1_read': _L0_attn_in['w1_read'], 'L0_attn_w2_read': _L0_attn_in['w2_read'], 'L0_attn_geo_w': _L0_attn_in['geo_w'], 'L0_attn_geo_b': _L0_attn_in['geo_b'], 'L0_attn_gate_w': _L0_attn_in['gate_w'], 'L0_attn_gate_b': _L0_attn_in['gate_b'], 'L0_attn_inc_scale': _L0_attn_in['inc_scale'], 'L0_attn_out_w': _L0_attn_in['out_w'], 'L0_attn_out_b': _L0_attn_in['out_b'], 'L0_ffn_w_gate': _L0_ffn_in['w_gate'], 'L0_ffn_w_up': _L0_ffn_in['w_up'], 'L0_ffn_w_down': _L0_ffn_in['w_down']}
    _x0 = _d['L0_attn_x']
    _d['L0_attn_x'] = jax.random.normal(jax.random.fold_in(jax.random.key(seed), 1), (2, 2048, 256), dtype=_x0.dtype)
    del _x0
    return _d

def reference(L0_attn_x, L0_attn_qkv_w, L0_attn_qkv_b, L0_attn_w1_write, L0_attn_w2_write, L0_attn_w1_read, L0_attn_w2_read, L0_attn_geo_w, L0_attn_geo_b, L0_attn_gate_w, L0_attn_gate_b, L0_attn_inc_scale, L0_attn_out_w, L0_attn_out_b, L0_ffn_w_gate, L0_ffn_w_up, L0_ffn_w_down):

    def _L0_attn_ref(x, qkv_w, qkv_b, w1_write, w2_write, w1_read, w2_read, geo_w, geo_b, gate_w, gate_b, inc_scale, out_w, out_b):
        import jax, jax.numpy as jnp
        import numpy as np
        _J6 = jnp.array([[0, 0, 0, 0, 0, 1], [0, 0, 0, 0, -1, 0], [0, 0, 0, 1, 0, 0], [0, 0, 1, 0, 0, 0], [0, -1, 0, 0, 0, 0], [1, 0, 0, 0, 0, 0]], dtype=jnp.float32)
        _PAIRS4 = [(0, 1), (0, 2), (0, 3), (1, 2), (1, 3), (2, 3)]

        def exterior(p1, p2):
            parts = [p1[..., i] * p2[..., j] - p1[..., j] * p2[..., i] for i, j in _PAIRS4]
            L = jnp.stack(parts, axis=-1)
            n = jnp.sqrt(jnp.sum(L * L, axis=-1, keepdims=True))
            return L / jnp.maximum(n, 1e-12)
        B, T, D = x.shape
        H = inc_scale.shape[0]
        dh = D // H
        scale = dh ** (-0.5)
        qkv = (x @ qkv_w + qkv_b).reshape(B, T, 3, H, dh)
        qkv = jnp.transpose(qkv, (2, 0, 3, 1, 4))
        q, k, v = (qkv[0], qkv[1], qkv[2])
        std_logits = jnp.einsum('bhqd,bhkd->bhqk', q, k) * scale
        x_prev = jnp.concatenate([jnp.zeros((B, 1, D), dtype=x.dtype), x[:, :-1]], axis=1)
        w1 = (x_prev @ w1_write).reshape(B, T, H, 4)
        w2 = (x @ w2_write).reshape(B, T, H, 4)
        write_lines = exterior(w1, w2)
        r1 = (x @ w1_read).reshape(B, T, H, 4)
        r2 = (x @ w2_read).reshape(B, T, H, 4)
        read_lines = exterior(r1, r2)
        J_write = jnp.einsum('bthi,ij->bthj', write_lines, _J6)
        geo_logits = jnp.einsum('bqhi,bkhi->bhqk', read_lines, J_write)
        geo_logits = geo_logits * inc_scale.reshape(1, H, 1, 1)
        mask = jnp.triu(jnp.ones((T, T), dtype=bool), k=1)
        neg = jnp.float32(-jnp.inf)
        std_attn = jax.nn.softmax(jnp.where(mask, neg, std_logits), axis=-1)
        std_out = jnp.einsum('bhqk,bhkd->bqhd', std_attn, v).reshape(B, T, D)
        geo_attn = jax.nn.softmax(jnp.where(mask, neg, geo_logits), axis=-1)
        geo_v = (x @ geo_w + geo_b).reshape(B, T, H, dh)
        geo_out = jnp.einsum('bhqk,bkhd->bqhd', geo_attn, geo_v).reshape(B, T, D)
        gate = jax.nn.sigmoid(x @ gate_w + gate_b)
        gate = jnp.mean(gate, axis=-1, keepdims=True)
        combined = (1.0 - gate) * std_out + gate * geo_out
        return combined @ out_w + out_b

    def _L0_ffn_ref(x, w_gate, w_up, w_down):
        import jax, jax.numpy as jnp
        import numpy as np
        DIM = 256
        HIDDEN = 768
        SCALE = 1.0 / 127.0

        def _dequant(w_int, dtype):
            return w_int.astype(dtype) * jnp.asarray(SCALE, dtype)
        wg = _dequant(w_gate, x.dtype)
        wu = _dequant(w_up, x.dtype)
        wd = _dequant(w_down, x.dtype)
        gate = jnp.einsum('bsd,hd->bsh', x, wg)
        up = jnp.einsum('bsd,hd->bsh', x, wu)
        h = jax.nn.silu(gate) * up
        return jnp.einsum('bsh,dh->bsd', h, wd)
    x = L0_attn_x
    x = _layernorm(x + _L0_attn_ref(x, L0_attn_qkv_w, L0_attn_qkv_b, L0_attn_w1_write, L0_attn_w2_write, L0_attn_w1_read, L0_attn_w2_read, L0_attn_geo_w, L0_attn_geo_b, L0_attn_gate_w, L0_attn_gate_b, L0_attn_inc_scale, L0_attn_out_w, L0_attn_out_b), axis=-1)
    x = _layernorm(x + _L0_ffn_ref(x, L0_ffn_w_gate, L0_ffn_w_up, L0_ffn_w_down), axis=-1)
    return x

_drawn_inputs = setup_inputs


def setup_inputs(seed=0):
    import zlib

    import numpy as np

    out = dict(_drawn_inputs(seed))
    spreads = {'L0_attn_qkv_b': (0.0, 0.383),
     'L0_attn_geo_b': (0.0, 0.36),
     'L0_attn_gate_b': (0.0, 2.0),
     'L0_attn_inc_scale': (1.0, 0.6),
     'L0_attn_out_b': (0.0, 0.1)}
    factors = {'L0_attn_qkv_w': 8.0,
     'L0_attn_w1_write': 8.0,
     'L0_attn_w2_write': 8.0,
     'L0_attn_w1_read': 8.0,
     'L0_attn_w2_read': 8.0,
     'L0_attn_geo_w': 8.0,
     'L0_attn_gate_w': 8.0}
    for name, (base, spread) in spreads.items():
        noise = np.random.default_rng([zlib.crc32(name.encode()), seed]).standard_normal(out[name].shape)
        drawn = base * np.exp(spread * noise) if base else spread * noise
        out[name] = jnp.asarray(drawn.astype(out[name].dtype))
    for name, factor in factors.items():
        out[name] = (out[name] * factor).astype(out[name].dtype)
    return out
```

```python
import concourse.bass as bass
from concourse import mybir
from contextlib import ExitStack

F32 = mybir.dt.float32
BF16 = mybir.dt.bfloat16
I32 = mybir.dt.int32
ALU = mybir.AluOpType
ACT = mybir.ActivationFunctionType
AX = mybir.AxisListType

P = 128
B, T, D, H = 2, 2048, 256, 16
DH = D // H
HID = 768
NK = D // P
CH = 512
NC = B * T // CH
CPB = T // CH
TT = CH // P
NPART = 3
PAIRS = [(0, 1), (0, 2), (0, 3), (1, 2), (1, 3), (2, 3)]
NCOMP = len(PAIRS)
J_SIGN = [1, -1, 1, 1, -1, 1]
SCALE_Q = float(DH) ** -0.5
SCALE_W = 1.0 / 127.0
EPS = 1e-5
MASKED = -1.0e38

HG = 4
NG = H // HG
ITEMS = 2 * B * NG
NKB = T // P
NQT = T // CH
Q_PARTS = [0, 0, 1, 1, 0, 2]
K_PARTS = [0, 1, 0, 1, 2, 0]
NROW = DH * len(Q_PARTS)
NROWM = NROW + 2
VW = 32


def steps():
    out = []
    for qt in range(NQT):
        for kb in range(0, TT * qt, 2):
            out.append((qt, [(kb, CH), (kb + 1, CH)]))
        for j in (0, 2):
            out.append((qt, [(TT * qt + j, CH - P * j), (TT * qt + j + 1, CH - P * (j + 1))]))
    return out


STEPS = steps()
NSTEP = len(STEPS)
NEX = NSTEP * HG
FIRST_OF = {qt: min(s for s, x in enumerate(STEPS) if x[0] == qt) for qt in range(NQT)}
LAST_OF = {qt: max(s for s, x in enumerate(STEPS) if x[0] == qt) for qt in range(NQT)}


def place(s):
    (_, w0), (_, w1) = STEPS[s][1]
    second = CH if w0 + w1 > CH else w0
    return (0, second), second + w1


def max_tiles():
    out = []
    for h in range(HG):
        for qb in range(NKB):
            end = (qb + 1) * P
            for k0 in range(0, end, CH):
                out.append((h, qb, k0, min(CH, end - k0), k0 + CH >= end))
    return out


MAXT = max_tiles()
NMT = len(MAXT)
NMX = NMT + 1
MAX_PER_STEP = 10
MAX_FIRST = 2


def max_of_step(s):
    a = (s - MAX_FIRST) * MAX_PER_STEP
    return list(range(max(a, 0), min(a + MAX_PER_STEP, NMT))) if s >= MAX_FIRST else []


MT_STEP = MAX_FIRST + -(-NMT // MAX_PER_STEP)
assert MT_STEP < NSTEP


def build(nc, xt, x, w_qk, b_qk, w_v, w_line, b_v, b_gate, inc, out_w, out_b, wg, wu, wd, out):
    ctx = ExitStack()
    with ctx:
        parts = nc.dram_tensor("parts", (2, 2, B, NPART, H * DH, T), BF16).ap()
        values = nc.dram_tensor("values", (ITEMS, P, NKB, HG * VW), F32).ap()
        heads = nc.dram_tensor("heads", (ITEMS, P, NKB, HG * DH), F32).ap()

        def sb(name, shape, dt=F32):
            return ctx.enter_context(nc.sbuf_tensor(name, shape, dt))

        ident = sb("ident", [P, P])
        ident16 = sb("ident16", [P, P], BF16)
        mask_kq = sb("mask_kq", [P, P], BF16)
        mask_qk = sb("mask_qk", [P, P], BF16)
        gate_z = sb("gate_z", [P, NC * TT, H])
        project(nc, xt, w_qk, b_qk, w_v, w_line, b_v, b_gate, inc, parts, values,
                ident, ident16, mask_kq, mask_qk, gate_z)
        attend(nc, parts, values, heads, ident, ident16, mask_kq, mask_qk)
        finish(nc, x, heads, gate_z, ident, out_w, out_b, wg, wu, wd, out)


def project(nc, xt, w_qk, b_qk, w_v, w_line, b_v, b_gate, inc, parts, values,
            ident, ident16, mask_kq, mask_qk, gate_z):
    LN_WRITES = 1 + NCOMP
    NR = 8
    LINE = 4 * H * 4
    NLN = TT * 2 * H
    with ExitStack() as ctx:
        def sb(name, shape, dt=F32):
            return ctx.enter_context(nc.sbuf_tensor(name, shape, dt))

        def pb(name, shape):
            return ctx.enter_context(nc.psum_tensor(name, shape, F32))

        def sem(name):
            return ctx.enter_context(nc.semaphore(name))

        wqk = sb("wqk", [P, NK, 2 * D])
        wv = sb("wv", [P, NK, 2 * D])
        wl = sb("wl", [P, NK, LINE + H])
        bqk = sb("bqk", [P, 4])
        bqs = sb("bqs", [P, 4])
        bv = sb("bv", [P, 2 * D])
        bg = sb("bg", [P, H])
        incb = sb("incb", [P, H])
        xc = [sb(f"xc{i}", [P, NK, CH + 1]) for i in range(2)]
        vn = [sb(f"vn{i}", [P, 2 * H, VW]) for i in range(2)]
        gs = sb("gs", [P, 2, TT * 2, H * 4])
        gz = sb("gz", [P, TT, H])
        prod_a = sb("prod_a", [P, NLN, NCOMP])
        prod_b = sb("prod_b", [P, NLN, NCOMP])
        line = sb("line", [P, NLN, NCOMP])
        sq = sb("sq", [P, NLN, NCOMP])
        sum6 = sb("sum6", [P, NLN])
        ss = sb("ss", [P, NLN])
        nrm = sb("nrm", [P, NLN])
        rn = sb("rn", [P, TT, 2, H])
        rinc = sb("rinc", [P, TT, H])
        rneg = sb("rneg", [P, TT, H])
        ln = sb("ln", [P, TT, 2, H, DH])
        t32 = [sb(f"t32_{i}", [P, CH]) for i in range(2)]
        d32 = [sb(f"d32_{i}", [P, CH]) for i in range(2)]
        sp3 = [sb(f"sp3_{i}", [P, NPART, CH], BF16) for i in range(2)]
        pn = [pb(f"pn{i}", [P, 2, CH]) for i in range(2)]
        pr = [pb(f"pr{i}", [P, CH]) for i in range(4)]

        w_in = sem("w_in")
        x_in = [sem(f"x_in{i}") for i in range(2)]
        n_ready = sem("n_ready")
        v_out = sem("v_out")
        g_out = sem("g_out")
        v_st = [sem(f"v_st{i}") for i in range(2)]
        rows_ready = sem("rows_ready")
        row_act = sem("row_act")
        d_done = sem("d_done")
        p2_done = sem("p2_done")
        p3_done = sem("p3_done")
        s_st = [sem(f"s_st{i}") for i in range(2)]
        ss_ready = sem("ss_ready")
        nrm_ready = sem("nrm_ready")
        ln_ready = sem("ln_ready")
        zero_ready = sem("zero_ready")
        id_ready = sem("id_ready")
        passed = sem("sp_passed1")
        dve = sem("dve")
        block = ctx.enter_context(nc.Block())

        @block.sync
        def _(q):
            q.dma_start(xc[0][:, :, :], xt[0].rearrange("(k p) t -> p k t", p=P)).then_inc(x_in[0], 16)
            q.dma_start(wv[:, :, :], w_v.rearrange("(k p) n -> p k n", p=P)).then_inc(w_in, 16)
            q.dma_start(wl[:, :, :], w_line.rearrange("(k p) n -> p k n", p=P)).then_inc(w_in, 16)
            q.dma_start(wqk[:, :, :], w_qk.rearrange("(k p) n -> p k n", p=P)).then_inc(w_in, 16)
            q.dma_start(xc[1][:, :, :], xt[1].rearrange("(k p) t -> p k t", p=P)).then_inc(x_in[1], 16)

            def stores(c, par):
                for tt in range(TT):
                    q.wait_ge(v_out, c * TT + tt + 1)
                    q.sem_inc(passed, 1)
                    dst = values[:, :, :, :].rearrange("(a b g) p k n -> a b k p g n", a=2, b=B)
                    for a in range(2):
                        q.dma_start(
                            dst[a, c // CPB, (c % CPB) * TT + tt, :, :, :],
                            vn[tt % 2][:, a * H:(a + 1) * H, :].rearrange("p (g h) w -> p g (h w)", g=NG)
                        ).then_inc(v_st[tt % 2], 16)
                for m in range(NR):
                    q.wait_ge(p3_done, c * NR + m + 1)
                    q.sem_inc(passed, 1)
                    q.dma_start(
                        parts[(m // 2) % 2, m // 4, c // CPB, :, (m % 2) * P:(m % 2 + 1) * P,
                              bass.ds((c % CPB) * CH, CH)].rearrange("s r t -> r s t"),
                        sp3[m % 2][:, :, :]).then_inc(s_st[m % 2], 16)

            def load_x(c, par):
                q.wait_ge(rows_ready, (c - 2) * NR + 4)
                q.sem_inc(passed, 1)
                q.dma_start(xc[par][:, :, :], xt[c].rearrange("(k p) t -> p k t", p=P)).then_inc(x_in[par], 16)

            with q.Fori(0, NC // 2 - 1) as k:
                for par in range(2):
                    load_x(2 * k + par + 2, par)
                    stores(2 * k + par, par)
            for c in (NC - 2, NC - 1):
                stores(c, c % 2)
            for i in range(2):
                q.wait_ge(v_st[i], NC * TT // 2 * 32)
                q.wait_ge(s_st[i], NC * NR // 2 * 16)

        @block.gpsimd
        def _(g):
            g.memset(ident[:, :], 0.0).then_inc(id_ready, 1)
            g.memset(ident16[:, :], 0.0).then_inc(id_ready, 1)
            g.memset(mask_kq[:, :], 0.0).then_inc(id_ready, 1)
            g.memset(mask_qk[:, :], 0.0).then_inc(id_ready, 1)
            for i in range(2):
                g.memset(vn[i][:, :, :], 0.0).then_inc(id_ready, 1)
            g.memset(ln[:, :, :, :, :], 0.0).then_inc(id_ready, 1)
            g.wait_ge(id_ready, 7)
            for i in range(2):
                g.memset(vn[i][:, :, DH:DH + 1], 1.0).then_inc(zero_ready, 1)
            for m in (ident, ident16):
                g.affine_select(out=m[:, :], in_=m[:, :], compare_op=ALU.not_equal, fill=1.0, base=0,
                                pattern=[[-1, P]], channel_multiplier=1).then_inc(id_ready, 1)
            g.affine_select(out=mask_kq[:, :], in_=mask_kq[:, :], compare_op=ALU.is_ge, fill=MASKED,
                            base=0, pattern=[[1, P]], channel_multiplier=-1).then_inc(id_ready, 1)
            g.affine_select(out=mask_qk[:, :], in_=mask_qk[:, :], compare_op=ALU.is_ge, fill=MASKED,
                            base=0, pattern=[[-1, P]], channel_multiplier=1).then_inc(id_ready, 1)
            with g.Fori(0, NC // 2) as k:
                for par in range(2):
                    for m in range(NR):
                        g.wait_ge(p2_done, (2 * k + par) * NR + m + 1)
                        g.tensor_tensor(out=sp3[m % 2][:, 2, :], in0=d32[m % 2][:, :],
                                        in1=sp3[m % 2][:, 1, :], op=ALU.subtract).then_inc(p3_done, 1)

        @block.tensor
        def _(pe):
            pe.wait_ge(w_in, 7 * 16)
            pe.wait_ge(id_ready, 11)

            def chunk(c, par, first):
                pe.wait_ge(x_in[par], (c // 2) * 16 + 16 if isinstance(c, int) else first)
                for tt in range(TT):
                    if not (isinstance(c, int) and c == 0 and tt < 2):
                        pe.wait_ge(v_out, c * TT + tt - 1)
                        pe.wait_ge(g_out, (c * TT + tt - 1) * 2)
                    tok = slice(1 + tt * P, 1 + (tt + 1) * P)
                    prev = slice(tt * P, (tt + 1) * P)
                    bank = pn[tt % 2]
                    for k in range(NK):
                        pe.matmul(bank[:, 0, :], xc[par][:, k, tok], wv[:, k, :], start=k == 0, stop=k == NK - 1)
                    for k in range(NK):
                        pe.matmul(bank[:, 1, 0:H * 4], xc[par][:, k, prev], wl[:, k, 0:H * 4],
                                  start=k == 0, stop=k == NK - 1)
                    for k in range(NK):
                        last = pe.matmul(bank[:, 1, H * 4:LINE + H], xc[par][:, k, tok], wl[:, k, H * 4:],
                                         start=k == 0, stop=k == NK - 1)
                    last.then_inc(n_ready, 1)
                for m in range(NR):
                    if not (isinstance(c, int) and c == 0 and m < 4):
                        pe.wait_ge(row_act, (c * NR + m - 3) * 2)
                    if m < 4:
                        for k in range(NK):
                            last = pe.matmul(pr[m % 4][:, :], wqk[:, k, m * P:(m + 1) * P], xc[par][:, k, 1:],
                                             start=k == 0, stop=k == NK - 1)
                        last.then_inc(rows_ready, 1)
                    else:
                        if m == 4:
                            pe.wait_ge(ln_ready, (c + 1) * LN_WRITES)
                        for tt in range(TT):
                            src = ln[:, tt, (m - 4) // 2, (m % 2) * 8:(m % 2) * 8 + 8, :]
                            last = pe.transpose(pr[m % 4][:, tt * P:(tt + 1) * P],
                                                src.rearrange("p h d -> p (h d)"), ident[:, :])
                        last.then_inc(rows_ready, 1)

            chunk(0, 0, None)
            chunk(1, 1, None)
            with pe.Fori(1, NC // 2) as k:
                for par in range(2):
                    chunk(2 * k + par, par, k * 16 + 16)

        @block.scalar
        def _(act):
            act.dma_start(bqk[:, :], b_qk).then_inc(w_in, 16)
            act.dma_start(bv[:, :], b_v.partition_broadcast(P)).then_inc(w_in, 16)
            act.dma_start(bg[:, :], b_gate.partition_broadcast(P)).then_inc(w_in, 16)
            act.dma_start(incb[:, :], inc.partition_broadcast(P)).then_inc(w_in, 16)
            act.wait_ge(dve, 2)

            def row_in(c, m, head):
                bias = bqs[:, m:m + 1] if m < 4 else 0.0
                scale = SCALE_Q if m < 2 else 1.0
                act.wait_ge(rows_ready, c * NR + m + 1)
                if not (head and m < 2):
                    act.wait_ge(d_done, c * NR + m - 1)
                    act.wait_ge(s_st[m % 2], (c * (NR // 2) + m // 2) * 16)
                act.activation(t32[m % 2][:, :], pr[m % 4][:, :], ACT.Identity, bias=bias, scale=scale)\
                   .then_inc(row_act, 1)
                act.activation(sp3[m % 2][:, 0, :], pr[m % 4][:, :], ACT.Identity, bias=bias, scale=scale)\
                   .then_inc(row_act, 1)

            def second_part(c, m):
                act.wait_ge(d_done, c * NR + m + 1)
                act.activation(sp3[m % 2][:, 1, :], d32[m % 2][:, :], ACT.Copy).then_inc(p2_done, 1)

            def chunk(c, head):
                for tt in range(TT):
                    act.wait_ge(n_ready, c * TT + tt + 1)
                    if tt == 0 and not head:
                        act.wait_ge(ln_ready, c * LN_WRITES)
                    bank = pn[tt % 2][:, 1, :]
                    act.activation(gs[:, :, 2 * tt:2 * tt + 2, :],
                                   bank[:, 0:LINE].rearrange("p (y w n) -> p w y n", y=2, w=2),
                                   ACT.Copy).then_inc(g_out, 1)
                    act.activation(gz[:, tt, :], bank[:, LINE:LINE + H], ACT.Copy).then_inc(g_out, 1)
                for m in range(NR):
                    row_in(c, m, head)
                    if m == 1:
                        act.wait_ge(ss_ready, c + 1)
                        act.activation(nrm[:, :], ss[:, :], ACT.Sqrt).then_inc(nrm_ready, 1)
                    if m >= 1:
                        second_part(c, m - 1)
                second_part(c, NR - 1)

            chunk(0, True)
            with act.Fori(1, NC) as c:
                chunk(c, False)

        @block.vector
        def _(v):
            v.wait_ge(w_in, 7 * 16)
            v.tensor_scalar(bqs[:, 0:2], bqk[:, 0:2], SCALE_Q, None, ALU.mult).then_inc(dve, 1)
            v.tensor_copy(bqs[:, 2:4], bqk[:, 2:4]).then_inc(dve, 1)
            v.wait_ge(zero_ready, 2)
            v.wait_ge(id_ready, 11)
            p1, p2 = (gs[:, w, :, :].rearrange("p y (h c) -> p (y h) c", c=4) for w in range(2))
            line_v = line[:, :, :].rearrange("p (t y h) c -> p t y h c", t=TT, y=2)
            LINKS = 7

            def chunk(c, head):
                base = c * LINKS + 2
                for tt in range(TT):
                    v.wait_ge(n_ready, c * TT + tt + 1)
                    if not (head and tt < 2):
                        v.wait_ge(v_st[tt % 2], (c * (TT // 2) + tt // 2) * 32)
                    v.tensor_tensor(out=vn[tt % 2][:, :, 0:DH],
                                    in0=pn[tt % 2][:, 0, :].rearrange("p (h d) -> p h d", d=DH),
                                    in1=bv[:, :].rearrange("p (h d) -> p h d", d=DH),
                                    op=ALU.add).then_inc(v_out, 1)
                v.wait_ge(g_out, (c + 1) * TT * 2)
                v.tensor_tensor(out=gate_z[:, bass.ds(c * TT, TT), :], in0=gz[:, :, :],
                                in1=bg[:, :].unsqueeze(1).to_broadcast([P, TT, H]), op=ALU.add)
                o = 0
                for i in range(3):
                    n = 3 - i
                    v.tensor_tensor(out=prod_a[:, :, o:o + n], in0=p1[:, :, i:i + 1].to_broadcast([P, NLN, n]),
                                    in1=p2[:, :, i + 1:4], op=ALU.mult)
                    last = v.tensor_tensor(out=prod_b[:, :, o:o + n], in0=p1[:, :, i + 1:4],
                                           in1=p2[:, :, i:i + 1].to_broadcast([P, NLN, n]), op=ALU.mult)
                    o += n
                last.then_inc(dve, 1)
                v.wait_ge(dve, base + 1)
                v.tensor_tensor(out=line[:, :, :], in0=prod_a[:, :, :], in1=prod_b[:, :, :],
                                op=ALU.subtract).then_inc(dve, 1)
                v.wait_ge(dve, base + 2)
                v.tensor_tensor(out=sq[:, :, :], in0=line[:, :, :], in1=line[:, :, :], op=ALU.mult)\
                 .then_inc(dve, 1)
                v.wait_ge(dve, base + 3)
                v.tensor_reduce(out=sum6[:, :], in_=sq[:, :, :], axis=AX.X, op=ALU.add).then_inc(dve, 1)
                v.wait_ge(dve, base + 4)
                if not head:
                    v.wait_ge(nrm_ready, c)
                v.tensor_scalar(ss[:, :], sum6[:, :], 1e-24, None, ALU.max).then_inc(ss_ready, 1)
                v.wait_ge(nrm_ready, c + 1)
                v.reciprocal(rn[:, :, :, :].rearrange("p t y h -> p (t y h)"), nrm[:, :]).then_inc(dve, 1)
                v.wait_ge(dve, base + 5)
                v.tensor_tensor(out=rinc[:, :, :], in0=rn[:, :, 1, :],
                                in1=incb[:, :].unsqueeze(1).to_broadcast([P, TT, H]), op=ALU.mult)\
                 .then_inc(dve, 1)
                v.wait_ge(dve, base + 6)
                v.tensor_scalar(rneg[:, :, :], rinc[:, :, :], -1.0, None, ALU.mult).then_inc(dve, 1)
                v.wait_ge(dve, base + 7)
                if not head:
                    v.wait_ge(rows_ready, c * NR)
                v.tensor_tensor(
                    out=ln[:, :, 1, :, 0:NCOMP], in0=line_v[:, :, 0, :, :],
                    in1=rn[:, :, 0, :].unsqueeze(3).to_broadcast([P, TT, H, NCOMP]),
                    op=ALU.mult).then_inc(ln_ready, 1)
                for i in range(NCOMP):
                    v.tensor_tensor(out=ln[:, :, 0, :, NCOMP - 1 - i], in0=line_v[:, :, 1, :, i],
                                    in1=(rinc if J_SIGN[i] > 0 else rneg)[:, :, :],
                                    op=ALU.mult).then_inc(ln_ready, 1)
                for m in range(NR):
                    v.wait_ge(row_act, (c * NR + m + 1) * 2)
                    if not (head and m < 2):
                        v.wait_ge(p3_done, c * NR + m - 1)
                    v.tensor_tensor(out=d32[m % 2][:, :], in0=t32[m % 2][:, :], in1=sp3[m % 2][:, 0, :],
                                    op=ALU.subtract).then_inc(d_done, 1)

            chunk(0, True)
            with v.Fori(1, NC) as c:
                chunk(c, False)


def attend(nc, parts, values, heads, ident, ident16, mask_kq, mask_qk):
    with ExitStack() as ctx:
        def sb(name, shape, dt=F32):
            return ctx.enter_context(nc.sbuf_tensor(name, shape, dt))

        def pb(name, shape):
            return ctx.enter_context(nc.psum_tensor(name, shape, F32))

        def sem(name):
            return ctx.enter_context(nc.semaphore(name))

        qa = [sb(f"qa{i}", [P, HG, T], BF16) for i in range(2)]
        ka = [sb(f"ka{i}", [P, HG, T], BF16) for i in range(2)]
        va = [sb(f"va{i}", [P, NKB, HG * VW]) for i in range(2)]
        prob = [sb(f"prob{i}", [P, 2 * CH]) for i in range(8)]
        ot = [sb(f"ot{i}", [P, CH]) for i in range(2)]
        rz = sb("rz", [P, TT * HG])
        on = [sb(f"on{i}", [P, TT, HG * DH]) for i in range(2)]
        mp = [sb(f"mp{i}", [P, HG * NKB, NKB * P // CH]) for i in range(2)]
        negm = sb("negm", [P, P])
        mrow = sb("mrow", [HG * NKB, 2, P], BF16)
        ex = pb("ex", [P, 2, 2 * CH])
        mx = pb("mx", [P, 2, CH])
        pv = pb("pv", [P, 2, CH])

        qk_in = [[sem(f"qk_in{i}_{j}") for j in range(2)] for i in range(2)]
        v_in = [sem(f"v_in{i}") for i in range(2)]
        m_in = sem("m_in")
        ones_ready = sem("ones_ready")
        ex_ready = sem("ex_ready")
        ex_done = sem("ex_done")
        pv_step = sem("pv_step")
        ot_ready = sem("ot_ready")
        tr_done = sem("tr_done")
        rz_ready = sem("rz_ready")
        on_ready = sem("on_ready")
        on_st = [sem(f"on_st{i}") for i in range(2)]
        mx_ready = sem("mx_ready")
        mx_free = sem("mx_free")
        negm_ready = sem("negm_ready")
        m_hi = sem("m_hi")
        passed = sem("sp_passed2")
        block = ctx.enter_context(nc.Block())

        @block.sync
        def _(q):
            def load_qk(it, par):
                a, b, g = it // (B * NG), (it // NG) % B, it % NG
                for j in range(2):
                    for side, dst, order in ((0, qa, Q_PARTS), (1, ka, K_PARTS)):
                        for n, s in enumerate(order):
                            src = parts[side, a, b, s, bass.ds(g * (HG * DH) + j * 2 * DH, 2 * DH), :]
                            q.dma_start(dst[par][n * DH:(n + 1) * DH, 2 * j:2 * j + 2, :],
                                        src.rearrange("(h d) t -> d h t", h=2)).then_inc(qk_in[par][j], 16)

            def load_v(it, par):
                q.dma_start(va[par][:, :, :], values[it]).then_inc(v_in[par], 16)

            def store(it, qt):
                q.wait_ge(on_ready, it * NQT + qt + 1)
                q.sem_inc(passed, 1)
                q.dma_start(heads[it, :, qt * TT:(qt + 1) * TT, :],
                            on[qt % 2][:, :, :]).then_inc(on_st[qt % 2], 16)

            def rows(it, par):
                q.wait_ge(mx_free, (it + 1) * NMX)
                for i in range(2):
                    q.dma_start(qa[par][NROW + i:NROW + i + 1, :, :].rearrange("p h (k t) -> p (h k) t", t=P),
                                mrow[:, i, :]).then_inc(m_in, 16)

            def item(it, par, has_prev, has_next):
                if has_next:
                    if has_prev:
                        q.wait_ge(ex_ready, it * NEX)
                        q.sem_inc(passed, 1)
                    load_qk(it + 1, 1 - par)
                if has_prev:
                    store(it - 1, NQT - 1)
                if has_next:
                    if has_prev:
                        q.wait_ge(pv_step, it * NSTEP)
                        q.sem_inc(passed, 1)
                    load_v(it + 1, 1 - par)
                for qt in range(NQT - 1):
                    store(it, qt)
                if has_next:
                    rows(it + 1, 1 - par)

            load_qk(0, 0)
            load_v(0, 0)
            rows(0, 0)
            item(0, 0, False, True)
            with q.Fori(0, ITEMS // 2 - 1) as k:
                item(2 * k + 1, 1, True, True)
                item(2 * k + 2, 0, True, True)
            item(ITEMS - 1, 1, True, False)
            store(ITEMS - 1, NQT - 1)
            for i in range(2):
                q.wait_ge(on_st[i], ITEMS * NQT // 2 * 16)

        @block.gpsimd
        def _(g):
            g.memset(negm[:, :], 0.0).then_inc(ones_ready, 1)
            for i in range(2):
                g.wait_ge(ones_ready, 2 * i + 1)
                g.memset(ka[i][NROW:NROWM, :, :], 1.0).then_inc(ones_ready, 1)
                g.wait_ge(ones_ready, 2 * i + 2)
                g.memset(mp[i][:, :, :], MASKED).then_inc(ones_ready, 1)

        @block.tensor
        def _(pe):
            pe.wait_ge(ones_ready, 5)

            def scores(it, par, s, h, head):
                n = s * HG + h
                slot = n % 2
                if not (head and n < 2):
                    pe.wait_ge(ex_done, it * NEX + n - 1)
                qt, blocks = STEPS[s]
                at, _ = place(s)
                for (kb, w), c0 in zip(blocks, at):
                    dst = ex[:, slot, c0:c0 + w]
                    on_diagonal = kb >= TT * qt
                    last = pe.matmul(dst, ka[par][0:NROWM, h, kb * P:(kb + 1) * P],
                                     qa[par][0:NROWM, h, (qt + 1) * CH - w:(qt + 1) * CH],
                                     start=True, stop=not on_diagonal)
                    if on_diagonal:
                        last = pe.matmul(dst[:, 0:P], ident16[:, :], mask_kq[:, :], start=False, stop=True)
                last.then_inc(ex_ready, 1)

            def max_tile(it, par, u, head):
                h, qb, k0, w, on_diagonal = MAXT[u]
                slot = (par + u) % 2
                if qb == 0 and h % 2 == 0:
                    pe.wait_ge(qk_in[par][h // 2], (it // 2 + 1) * 12 * 16)
                if not (head and u < 2):
                    pe.wait_ge(mx_free, it * NMX + u - 1)
                dst = mx[:, slot, 0:w]
                last = pe.matmul(dst, qa[par][0:NROW, h, qb * P:(qb + 1) * P],
                                 ka[par][0:NROW, h, k0:k0 + w], start=True, stop=not on_diagonal)
                if on_diagonal:
                    last = pe.matmul(dst[:, w - P:w], ident16[:, :], mask_qk[:, :], start=False, stop=True)
                last.then_inc(mx_ready, 1)

            def max_rows(it, par):
                pe.wait_ge(negm_ready, it + 1)
                pe.transpose(mx[:, (par + NMT) % 2, 0:P], negm[:, :], ident[:, :]).then_inc(mx_ready, 1)

            def times_v(it, par, s, j, head):
                qt, blocks = STEPS[s]
                kb, w = blocks[j]
                at, _ = place(s)
                if j == 0:
                    pe.wait_ge(ex_done, it * NEX + s * HG + HG)
                    if s == 0:
                        pe.wait_ge(v_in[par], (it // 2 + 1) * 16)
                    if s == FIRST_OF[qt] and not (head and qt < 2):
                        pe.wait_ge(on_ready, it * NQT + qt - 1)
                end = j == 1 and s == LAST_OF[qt]
                for h in range(HG):
                    last = pe.matmul(pv[h * VW:(h + 1) * VW, qt % 2, CH - w:CH],
                                     va[par][:, kb, h * VW:(h + 1) * VW],
                                     prob[(s * HG + h) % 8][:, at[j]:at[j] + w],
                                     start=kb == 0, stop=end, tile_position=(0, h * VW))
                if j == 1:
                    last.then_inc(pv_step, 1)

            def turn(it, qt):
                pe.wait_ge(ot_ready, it * NQT + qt + 1)
                for i in range(TT):
                    last = pe.transpose(pv[:, qt % 2, i * P:(i + 1) * P], ot[qt % 2][:, i * P:(i + 1) * P],
                                        ident[:, :])
                last.then_inc(tr_done, 1)

            def step(it, par, s, head, has_next):
                later = list(max_of_step(s)) if has_next else []

                def some(n):
                    for _ in range(min(n, len(later))):
                        max_tile(it + 1, 1 - par, later.pop(0), False)

                before = (it, par, s - 1) if s else (it - 1, 1 - par, NSTEP - 1)
                scores(it, par, s, 0, head)
                scores(it, par, s, 1, head)
                some(3)
                if not (head and s == 0):
                    times_v(*before, 0, head)
                scores(it, par, s, 2, head)
                some(2)
                scores(it, par, s, 3, head)
                some(2)
                if not (head and s == 0):
                    times_v(*before, 1, head)
                some(NMT)
                if has_next and s == MT_STEP:
                    max_rows(it + 1, 1 - par)
                if s >= 1:
                    for qt in range(NQT):
                        if s - 2 == LAST_OF[qt]:
                            turn(it, qt)
                    if s == 1 and not head:
                        turn(it - 1, NQT - 1)

            def item(it, par, head, has_next):
                pe.wait_ge(m_in, (it + 1) * 32)
                for s in range(NSTEP):
                    step(it, par, s, head, has_next)

            for u in range(NMT):
                max_tile(0, 0, u, True)
            max_rows(0, 0)
            item(0, 0, True, True)
            with pe.Fori(0, ITEMS // 2 - 1) as k:
                item(2 * k + 1, 1, False, True)
                item(2 * k + 2, 0, False, True)
            item(ITEMS - 1, 1, False, False)
            for j in range(2):
                times_v(ITEMS - 1, 1, NSTEP - 1, j, False)
            turn(ITEMS - 1, NQT - 1)

        @block.scalar
        def _(act):
            def item(it, head):
                for n in range(NEX):
                    s = n // HG
                    _, w = place(s)
                    act.wait_ge(ex_ready, it * NEX + n + 1)
                    if n % HG == 0 and not (head and s < 2):
                        act.wait_ge(pv_step, it * NSTEP + s - 1)
                    act.activation(prob[n % 8][:, 0:w], ex[:, n % 2, 0:w], ACT.Exp).then_inc(ex_done, 1)

            item(0, True)
            with act.Fori(1, ITEMS) as it:
                item(it, False)

        @block.vector
        def _(v):
            v.wait_ge(ones_ready, 5)

            def max_tile(it, par, u):
                h, qb, k0, w, _ = MAXT[u]
                v.wait_ge(mx_ready, it * NMX + u + 1)
                v.tensor_reduce(out=mp[par][:, h * NKB + qb, k0 // CH:k0 // CH + 1], in_=mx[:, (par + u) % 2, 0:w],
                                axis=AX.X, op=ALU.max).then_inc(mx_free, 1)

            def max_rows(it, par, head):
                v.wait_ge(mx_free, it * NMX + NMT)
                if not head:
                    v.wait_ge(mx_ready, it * NMX)
                v.tensor_reduce(out=negm[:, 0:HG * NKB], in_=mp[par][:, :, :], axis=AX.X, op=ALU.max, negate=True)\
                 .then_inc(negm_ready, 1)
                v.wait_ge(mx_ready, (it + 1) * NMX)
                if not head:
                    v.wait_ge(m_in, it * 32)
                src = mx[0:HG * NKB, (par + NMT) % 2, 0:P]
                v.tensor_copy(mrow[:, 0, :], src).then_inc(m_hi, 1)
                v.wait_ge(m_hi, it + 1)
                v.tensor_tensor(out=mrow[:, 1, :], in0=src, in1=mrow[:, 0, :], op=ALU.subtract).then_inc(mx_free, 1)

            def take(it, qt, head):
                v.wait_ge(pv_step, it * NSTEP + LAST_OF[qt] + 1)
                if not (head and qt < 2):
                    v.wait_ge(tr_done, it * NQT + qt - 1)
                v.tensor_copy(ot[qt % 2][:, :], pv[:, qt % 2, :]).then_inc(ot_ready, 1)

            def normalise(it, qt, head):
                v.wait_ge(tr_done, it * NQT + qt + 1)
                if not (head and qt < 2):
                    v.wait_ge(on_st[qt % 2], (it * (NQT // 2) + qt // 2) * 16)
                src = pv[:, qt % 2, :].rearrange("p (n w) -> p n w", w=VW)
                v.reciprocal(rz[:, :].unsqueeze(2), src[:, :, DH:DH + 1]).then_inc(rz_ready, 1)
                v.wait_ge(rz_ready, it * NQT + qt + 1)
                v.tensor_tensor(out=on[qt % 2][:, :, :].rearrange("p s (h d) -> p (s h) d", d=DH),
                                in0=src[:, :, 0:DH], in1=rz[:, :].unsqueeze(2).to_broadcast([P, TT * HG, DH]),
                                op=ALU.mult).then_inc(on_ready, 1)

            def item(it, par, head, has_next):
                for s in range(NSTEP):
                    if has_next:
                        for u in max_of_step(s):
                            max_tile(it + 1, 1 - par, u)
                    if s == 0 and not head:
                        take(it - 1, NQT - 1, False)
                    if has_next and s == MT_STEP:
                        max_rows(it + 1, 1 - par, False)
                    if s == 1 and not head:
                        normalise(it - 1, NQT - 1, False)
                    for qt in range(NQT):
                        if s - 1 == LAST_OF[qt]:
                            take(it, qt, head)
                        if s - 2 == LAST_OF[qt]:
                            normalise(it, qt, head)

            for u in range(NMT):
                max_tile(0, 0, u)
            max_rows(0, 0, True)
            item(0, 0, True, True)
            with v.Fori(0, ITEMS // 2 - 1) as k:
                item(2 * k + 1, 1, False, True)
                item(2 * k + 2, 0, False, True)
            item(ITEMS - 1, 1, False, False)
            take(ITEMS - 1, NQT - 1, False)
            normalise(ITEMS - 1, NQT - 1, False)


def finish(nc, x, heads, gate_z, ident, out_w, out_b, wg, wu, wd, out):
    NT = NC * TT
    NM = HID // P
    with ExitStack() as ctx:
        def sb(name, shape, dt=F32):
            return ctx.enter_context(nc.sbuf_tensor(name, shape, dt))

        def pb(name, shape):
            return ctx.enter_context(nc.psum_tensor(name, shape, F32))

        def sem(name):
            return ctx.enter_context(nc.semaphore(name))

        wo = sb("wo", [P, NK, D])
        ob = sb("ob", [P, D])
        wgi = sb("wgi", [P, NK, HID], I32)
        wui = sb("wui", [P, NK, HID], I32)
        wdi = sb("wdi", [P, NM, D], I32)
        wgf = sb("wgf", [P, NK, HID])
        wuf = sb("wuf", [P, NK, HID])
        wdf = sb("wdf", [P, NM, D])
        ez = sb("ez", [P, NT, H])
        gsum = sb("gsum", [P, NT])
        gate = sb("gate", [P, NT])
        omg = sb("omg", [P, NT])
        att = [[sb(f"att{a}_{i}", [P, TT, D]) for i in range(2)] for a in range(2)]
        xin = [sb(f"xin{i}", [P, TT, D]) for i in range(2)]
        mix = [sb(f"mix{i}", [P, TT, D]) for i in range(2)]
        ct = [sb(f"ct{i}", [P, NK, CH]) for i in range(2)]
        res = sb("res", [P, NT, D])
        rch = [sb(f"rch{i}", [P, TT, D]) for i in range(2)]
        stat = sb("stat", [P, TT, 6])
        mvc = sb("mvc", [P, TT, 2])
        mv = sb("mv", [P, NT, 2])
        std = sb("std", [P, NT])
        rstd = sb("rstd", [P, NT])
        sg = [sb(f"sg{i}", [P, CH]) for i in range(2)]
        ht = [sb(f"ht{i}", [P, NM, CH]) for i in range(2)]
        pt = pb("pt", [P, NK, CH])
        pg = [pb(f"pg{i}", [P, 2, CH]) for i in range(2)]
        po = [pb(f"po{i}", [P, CH]) for i in range(2)]

        w_in = sem("w_in3")
        att_in = [sem(f"att_in{i}") for i in range(2)]
        wf_ready = sem("wf_ready")
        e_ready = sem("e_ready")
        dve = sem("dve3")
        gate_ready = sem("gate_ready")
        xb_ready = sem("xb_ready")
        mix_tmp = sem("mix_tmp")
        mix_ready = sem("mix_ready")
        pt_ready = sem("pt_ready")
        ct_ready = sem("ct_ready")
        po_ready = sem("po_ready")
        res_ready = sem("res_ready")
        kept = sem("kept")
        st_ready = sem("st_ready")
        mvc_ready = sem("mvc_ready")
        mv_ready = sem("mv_ready")
        std_ready = sem("std_ready")
        rstd_ready = sem("rstd_ready")
        y_ready = sem("y_ready")
        pg_ready = sem("pg_ready")
        sg_ready = sem("sg_ready")
        ht_ready = sem("ht_ready")
        o_ready = sem("o_ready")
        o_st = sem("o_st")
        passed = sem("sp_passed3")
        v_passed = sem("v_passed")
        block = ctx.enter_context(nc.Block())

        x_v = x.rearrange("(c t p) n -> c p t n", p=P, t=TT)
        out_v = out.rearrange("(c t p) n -> c p t n", p=P, t=TT)
        heads_v = heads[:, :, :, :].rearrange("(a b g) p k n -> a b g p k n", a=2, b=B)

        @block.sync
        def _(q):
            q.dma_start(wo[:, :, :], out_w.rearrange("(k p) n -> p k n", p=P)).then_inc(w_in, 16)
            q.dma_start(ob[:, :], out_b.partition_broadcast(P)).then_inc(w_in, 16)
            q.dma_start(wgi[:, :, :], wg.rearrange("(k p) n -> p k n", p=P)).then_inc(w_in, 16)
            q.dma_start(wui[:, :, :], wu.rearrange("(k p) n -> p k n", p=P)).then_inc(w_in, 16)
            q.dma_start(wdi[:, :, :], wd.rearrange("(k p) n -> p k n", p=P)).then_inc(w_in, 16)

            def load(c, par):
                for a in range(2):
                    for g in range(NG):
                        q.dma_start(att[a][par][:, :, g * HG * DH:(g + 1) * HG * DH],
                                    heads_v[a, c // CPB, g, :, bass.ds((c % CPB) * TT, TT), :])\
                         .then_inc(att_in[par], 16)
                q.dma_start(xin[par][:, :, :], x_v[c]).then_inc(att_in[par], 16)

            load(0, 0)
            load(1, 1)
            with q.Fori(1, NC // 2) as k:
                for par in range(2):
                    q.wait_ge(res_ready, (2 * k + par - 1) * TT)
                    q.sem_inc(passed, 1)
                    load(2 * k + par, par)
            with q.Fori(0, NC) as c:
                q.wait_ge(o_ready, (c + 1) * TT)
                q.sem_inc(passed, 1)
                q.dma_start(out_v[c], res[:, bass.ds(c * TT, TT), :]).then_inc(o_st, 16)
            q.wait_ge(o_st, NC * 16)

        @block.gpsimd
        def _(g):
            def keep(c, par, base):
                g.wait_ge(res_ready, (base + c + 1) * TT)
                g.tensor_copy(res[:, bass.ds(c * TT, TT), :], rch[par][:, :, :]).then_inc(kept, 1)

            g.wait_ge(w_in, 5 * 16)
            with g.Fori(0, NC // 2) as k:
                for par in range(2):
                    g.wait_ge(att_in[par], (k + 1) * 9 * 16)
                    g.tensor_tensor(out=xin[par][:, :, :], in0=xin[par][:, :, :],
                                    in1=ob[:, :].unsqueeze(1).to_broadcast([P, TT, D]), op=ALU.add)\
                     .then_inc(xb_ready, 1)
                    keep(2 * k + par, par, 0)
            with g.Fori(0, NC // 2) as k:
                for par in range(2):
                    keep(2 * k + par, par, NC)

        @block.tensor
        def _(pe):
            pe.wait_ge(w_in, 5 * 16)

            def transposes(src, c):
                for k in range(NK):
                    for tt in range(TT):
                        last = pe.transpose(pt[:, k, tt * P:(tt + 1) * P], src(tt, k), ident[:, :])
                last.then_inc(pt_ready, 1)

            def out_chunk(c, par, head):
                pe.wait_ge(mix_ready, (c + 1) * TT)
                if not head:
                    pe.wait_ge(ct_ready, c)
                transposes(lambda tt, k: mix[par][:, tt, k * P:(k + 1) * P], c)
                pe.wait_ge(ct_ready, c + 1)
                for tt in range(TT):
                    if not (head and tt < 2):
                        pe.wait_ge(res_ready, c * TT + tt - 1)
                    for k in range(NK):
                        last = pe.matmul(po[tt % 2][:, 0:D], ct[par][:, k, tt * P:(tt + 1) * P], wo[:, k, :],
                                         start=k == 0, stop=k == NK - 1)
                    last.then_inc(po_ready, 1)

            out_chunk(0, 0, True)
            out_chunk(1, 1, False)
            with pe.Fori(1, NC // 2) as k:
                for par in range(2):
                    out_chunk(2 * k + par, par, False)

            def ffn_chunk(c, par, head):
                pe.wait_ge(y_ready, (c + 1) * TT)
                pe.wait_ge(ct_ready, NC + c)
                transposes(lambda tt, k: mix[par][:, tt, k * P:(k + 1) * P], c)
                pe.wait_ge(ct_ready, NC + c + 1)
                for m in range(NM):
                    if not (head and m < 2):
                        pe.wait_ge(ht_ready, c * NM + m - 1)
                    for i, w in enumerate((wgf, wuf)):
                        for k in range(NK):
                            last = pe.matmul(pg[m % 2][:, i, :], w[:, k, m * P:(m + 1) * P], ct[par][:, k, :],
                                             start=k == 0, stop=k == NK - 1)
                    last.then_inc(pg_ready, 1)
                pe.wait_ge(ht_ready, (c + 1) * NM)
                for tt in range(TT):
                    pe.wait_ge(res_ready, NT + c * TT + tt - 1)
                    for m in range(NM):
                        last = pe.matmul(po[tt % 2][:, 0:D], ht[par][:, m, tt * P:(tt + 1) * P], wdf[:, m, :],
                                         start=m == 0, stop=m == NM - 1)
                    last.then_inc(po_ready, 1)

            pe.wait_ge(wf_ready, 3)
            ffn_chunk(0, 0, True)
            ffn_chunk(1, 1, False)
            with pe.Fori(1, NC // 2) as k:
                for par in range(2):
                    ffn_chunk(2 * k + par, par, False)

        @block.scalar
        def _(act):
            act.activation(ez[:, :, :], gate_z[:, :, :], ACT.Exp, scale=-1.0).then_inc(e_ready, 1)

            def columns(c, par, base):
                act.wait_ge(pt_ready, base + c + 1)
                if not (isinstance(c, int) and c == 0 and base == 0):
                    act.wait_ge(po_ready, (base + c - 1) * TT) if not (isinstance(c, int) and base + c < 2) else None
                act.activation(ct[par][:, :, :], pt[:, :, :], ACT.Copy).then_inc(ct_ready, 1)

            columns(0, 0, 0)
            columns(1, 1, 0)
            with act.Fori(1, NC // 2) as k:
                for par in range(2):
                    columns(2 * k + par, par, 0)

            def root(n):
                act.wait_ge(mv_ready, n * (NC + 1))
                act.activation(std[:, :], mv[:, :, 1], ACT.Sqrt).then_inc(std_ready, 1)

            root(1)

            def ffn_chunk(c, par, head):
                columns(c, par, NC)
                for m in range(NM):
                    act.wait_ge(pg_ready, c * NM + m + 1)
                    if not (head and m < 2):
                        act.wait_ge(ht_ready, c * NM + m - 1)
                    act.activation(sg[m % 2][:, :], pg[m % 2][:, 0, :], ACT.Silu, scale=SCALE_W)\
                       .then_inc(sg_ready, 1)

            ffn_chunk(0, 0, True)
            ffn_chunk(1, 1, False)
            with act.Fori(1, NC // 2) as k:
                for par in range(2):
                    ffn_chunk(2 * k + par, par, False)
            root(2)

        @block.vector
        def _(v):
            v.wait_ge(e_ready, 1)
            v.tensor_scalar(ez[:, :, :], ez[:, :, :], 1.0, None, ALU.add).then_inc(dve, 1)
            v.wait_ge(dve, 1)
            v.reciprocal(ez[:, :, :], ez[:, :, :]).then_inc(dve, 1)
            v.wait_ge(dve, 2)
            v.tensor_reduce(out=gsum[:, :], in_=ez[:, :, :], axis=AX.X, op=ALU.add).then_inc(dve, 1)
            v.wait_ge(dve, 3)
            v.tensor_scalar(gate[:, :], gsum[:, :], 1.0 / H, None, ALU.mult).then_inc(gate_ready, 1)
            v.tensor_scalar(omg[:, :], gsum[:, :], -1.0 / H, 1.0, ALU.mult, ALU.add).then_inc(gate_ready, 1)
            v.wait_ge(gate_ready, 2)

            def mixed(c, par, head):
                v.wait_ge(att_in[par], (c // 2 + 1) * 9 * 16)
                if not head:
                    v.wait_ge(pt_ready, c - 1)
                for tt in range(TT):
                    n = c * TT + tt
                    v.tensor_scalar(mix[par][:, tt, :], att[0][par][:, tt, :], omg[:, bass.ds(n, 1)], None,
                                    ALU.mult).then_inc(mix_tmp, 1)
                v.wait_ge(mix_tmp, (c + 1) * TT)
                for tt in range(TT):
                    n = c * TT + tt
                    v.scalar_tensor_tensor(out=mix[par][:, tt, :], in0=att[1][par][:, tt, :],
                                           scalar=gate[:, bass.ds(n, 1)], in1=mix[par][:, tt, :],
                                           op0=ALU.mult, op1=ALU.add).then_inc(mix_ready, 1)

            def residual(c, par, base, head, scale):
                if not head:
                    v.wait_ge(kept, base // TT + c - 1)
                for tt in range(TT):
                    v.wait_ge(po_ready, base + c * TT + tt + 1)
                    if scale is None:
                        if tt == 0:
                            v.wait_ge(xb_ready, c + 1)
                        v.tensor_tensor(out=rch[par][:, tt, :], in0=po[tt % 2][:, 0:D], in1=xin[par][:, tt, :],
                                        op=ALU.add).then_inc(res_ready, 1)
                    else:
                        v.scalar_tensor_tensor(out=rch[par][:, tt, :], in0=po[tt % 2][:, 0:D], scalar=scale,
                                               in1=mix[par][:, tt, :], op0=ALU.mult, op1=ALU.add)\
                         .then_inc(res_ready, 1)
                v.wait_ge(res_ready, base + (c + 1) * TT)
                for tt in range(TT):
                    v.bn_stats(stat[:, tt, :], rch[par][:, tt, :]).then_inc(st_ready, 1)
                v.wait_ge(st_ready, base + (c + 1) * TT)
                v.sem_inc(v_passed, 1)
                for tt in range(TT):
                    last = v.bn_aggr(mvc[:, tt, :], stat[:, tt, :])
                last.then_inc(mvc_ready, 1)
                v.wait_ge(mvc_ready, base // TT + c + 1)
                v.tensor_copy(mv[:, bass.ds(c * TT, TT), :], mvc[:, :, :]).then_inc(mv_ready, 1)

            mixed(0, 0, True)
            mixed(1, 1, True)
            for c in range(2):
                residual(c, c, 0, True, None)
                mixed(c + 2, c, False)
            with v.Fori(1, NC // 2 - 1) as k:
                for par in range(2):
                    residual(2 * k + par, par, 0, False, None)
                    mixed(2 * k + par + 2, par, False)
            for c in (NC - 2, NC - 1):
                residual(c, c % 2, 0, False, None)

            def scales(n):
                v.wait_ge(mv_ready, n * (NC + 1) - 1)
                v.tensor_scalar(mv[:, :, 1], mv[:, :, 1], EPS, None, ALU.add).then_inc(mv_ready, 1)
                v.wait_ge(std_ready, n)
                v.reciprocal(rstd[:, :], std[:, :]).then_inc(rstd_ready, 1)
                v.wait_ge(rstd_ready, n)

            def norm(c, dst, done, base):
                v.wait_ge(kept, base + c + 1)
                for tt in range(TT):
                    n = c * TT + tt
                    v.tensor_scalar(dst(tt, n), res[:, bass.ds(n, 1), :].rearrange("p a n -> p (a n)"),
                                    mv[:, bass.ds(n, 1), 0:1].rearrange("p a n -> p (a n)"),
                                    rstd[:, bass.ds(n, 1)], ALU.subtract, ALU.mult).then_inc(done, 1)

            scales(1)
            v.wait_ge(w_in, 5 * 16)
            for wf, wi in ((wgf, wgi), (wuf, wui), (wdf, wdi)):
                v.tensor_copy(wf[:, :, :], wi[:, :, :]).then_inc(wf_ready, 1)

            def ffn_norm(c, par):
                norm(c, lambda tt, n: mix[par][:, tt, :], y_ready, 0)

            def ffn_chunk(c, par):
                for m in range(NM):
                    v.wait_ge(sg_ready, c * NM + m + 1)
                    v.scalar_tensor_tensor(out=ht[par][:, m, :], in0=pg[m % 2][:, 1, :], scalar=SCALE_W,
                                           in1=sg[m % 2][:, :], op0=ALU.mult, op1=ALU.mult).then_inc(ht_ready, 1)
                residual(c, par, NT, False, SCALE_W)

            ffn_norm(0, 0)
            ffn_norm(1, 1)
            with v.Fori(0, NC // 2 - 1) as k:
                for par in range(2):
                    c = 2 * k + par
                    ffn_chunk(c, par)
                    ffn_norm(c + 2, par)
            for c in (NC - 2, NC - 1):
                ffn_chunk(c, c % 2)
            scales(2)
            with v.Fori(0, NC) as c:
                norm(c, lambda tt, n: res[:, bass.ds(n, 1), :].rearrange("p a n -> p (a n)"), o_ready, NC)


_INPUTS = ("xt", "x", "w_qk", "b_qk", "w_v", "w_line", "b_v", "b_gate", "inc", "out_w", "out_b", "wg", "wu", "wd")


def kernel(**inputs):
    import numpy as np
    import concourse.bacc as bacc
    from concourse.bass_utils import run_bass_kernel_spmd as run

    a = {k[3:]: np.asarray(v) for k, v in inputs.items()}
    x = a["attn_x"].reshape(B * T, D)
    padded = np.zeros((B, D, T + 1), x.dtype)
    padded[:, :, 1:] = x.reshape(B, T, D).transpose(0, 2, 1)
    xt = np.stack([padded[c // CPB, :, (c % CPB) * CH:(c % CPB) * CH + CH + 1] for c in range(NC)])
    qkv_w, qkv_b = a["attn_qkv_w"], a["attn_qkv_b"]
    laid = {
        "xt": xt, "x": x,
        "w_qk": qkv_w[:, :2 * D], "b_qk": qkv_b[:2 * D].reshape(4, P).T,
        "w_v": np.concatenate([qkv_w[:, 2 * D:], a["attn_geo_w"]], 1),
        "w_line": np.concatenate([a["attn_w1_write"], a["attn_w2_write"], a["attn_w1_read"],
                                  a["attn_w2_read"], a["attn_gate_w"]], 1),
        "b_v": np.concatenate([qkv_b[2 * D:], a["attn_geo_b"]]), "b_gate": a["attn_gate_b"],
        "inc": a["attn_inc_scale"], "out_w": a["attn_out_w"], "out_b": a["attn_out_b"],
        "wg": a["ffn_w_gate"].T, "wu": a["ffn_w_up"].T, "wd": a["ffn_w_down"].T,
    }
    nc = bacc.Bacc("TRN2", target_bir_lowering=False, num_devices=1)
    arrays, args = {}, []
    for name in _INPUTS:
        arr = np.ascontiguousarray(laid[name])
        arrays[f"in_{name}"] = arr
        args.append(nc.dram_tensor(f"in_{name}", arr.shape, mybir.dt.from_np(arr.dtype), kind="ExternalInput").ap())
    out = nc.dram_tensor("out_0", (B * T, D), F32, kind="ExternalOutput").ap()
    build(nc, *args, out)
    r = run(nc, [arrays], core_ids=[0])
    return r.results[0]["out_0"].reshape(B, T, D)
```

```python
import concourse.bass as bass
from concourse import mybir
from contextlib import ExitStack

F32 = mybir.dt.float32
BF16 = mybir.dt.bfloat16
I32 = mybir.dt.int32
ALU = mybir.AluOpType
ACT = mybir.ActivationFunctionType
AX = mybir.AxisListType

P = 128
B, T, D, H = 2, 2048, 256, 16
DH = D // H
HID = 768
NK = D // P
CH = 512
NC = B * T // CH
CPB = T // CH
TT = CH // P
NPART = 3
PAIRS = [(0, 1), (0, 2), (0, 3), (1, 2), (1, 3), (2, 3)]
NCOMP = len(PAIRS)
J_SIGN = [1, -1, 1, 1, -1, 1]
SCALE_Q = float(DH) ** -0.5
SCALE_W = 1.0 / 127.0
EPS = 1e-5
MASKED = -1.0e38
GEO_SAFE = 60.0
GEO, DOT = 0, 1
ORDER = (1, 0)

HG = 4
NG = H // HG
ITEMS = 2 * B * NG
NKB = T // P
NQT = T // CH
Q_PARTS = [0, 0, 1, 1, 0, 2]
K_PARTS = [0, 1, 0, 1, 2, 0]
NROW = DH * len(Q_PARTS)
NROWM = NROW + 2
VW = 32


def steps():
    out = []
    for qt in range(NQT):
        for kb in range(0, TT * qt, 2):
            out.append((qt, [(kb, CH), (kb + 1, CH)]))
        for j in (0, 2):
            out.append((qt, [(TT * qt + j, CH - P * j), (TT * qt + j + 1, CH - P * (j + 1))]))
    return out


STEPS = steps()
NSTEP = len(STEPS)
NEX = NSTEP * HG
FIRST_OF = {qt: min(s for s, x in enumerate(STEPS) if x[0] == qt) for qt in range(NQT)}
LAST_OF = {qt: max(s for s, x in enumerate(STEPS) if x[0] == qt) for qt in range(NQT)}


def place(s):
    (_, w0), (_, w1) = STEPS[s][1]
    second = CH if w0 + w1 > CH else w0
    return (0, second), second + w1


def max_tiles():
    out = []
    for h in range(HG):
        for qb in range(NKB):
            end = (qb + 1) * P
            for k0 in range(0, end, CH):
                out.append((h, qb, k0, min(CH, end - k0), k0 + CH >= end))
    return out


MAXT = max_tiles()
NMT = len(MAXT)
NMX = NMT + 1
MAX_STEPS = (1, NSTEP - 2)
MT_STEP = NSTEP - 1


def spread():
    size = [sum(w for _, w in STEPS[s][1]) if MAX_STEPS[0] <= s <= MAX_STEPS[1] else 0 for s in range(NSTEP)]
    cols = [w + (P if d else 0) for _, _, _, w, d in MAXT]
    out, u, done = [], 0, 0
    for s in range(NSTEP):
        mine = []
        while u < NMT and done + cols[u] / 2 <= sum(cols) * sum(size[:s + 1]) / sum(size):
            mine.append(u)
            done += cols[u]
            u += 1
        out.append(mine)
    assert u == NMT
    return out


SPREAD = spread()


def build(nc, xt, x, w_qk, b_qk, w_v, w_line, b_v, b_gate, inc, out_w, out_b, wg, wu, wd, out):
    ctx = ExitStack()
    with ctx:
        parts = nc.dram_tensor("parts", (2, 2, B, NPART, H * DH, T), BF16).ap()
        values = nc.dram_tensor("values", (ITEMS, P, NKB, HG * VW), F32).ap()
        heads = nc.dram_tensor("heads", (ITEMS, P, NKB, HG * DH), F32).ap()

        def sb(name, shape, dt=F32):
            return ctx.enter_context(nc.sbuf_tensor(name, shape, dt))

        ident = sb("ident", [P, P])
        ident16 = sb("ident16", [P, P], BF16)
        mask_kq = sb("mask_kq", [P, P], BF16)
        mask_qk = sb("mask_qk", [P, P], BF16)
        gate_z = sb("gate_z", [P, NC * TT, H])
        wide = sb("wide", [P, 1], I32)
        project(nc, xt, w_qk, b_qk, w_v, w_line, b_v, b_gate, inc, parts, values,
                ident, ident16, mask_kq, mask_qk, gate_z, wide)
        attend(nc, parts, values, heads, ident, ident16, mask_kq, mask_qk, wide)
        finish(nc, x, heads, gate_z, ident, out_w, out_b, wg, wu, wd, out)


def project(nc, xt, w_qk, b_qk, w_v, w_line, b_v, b_gate, inc, parts, values,
            ident, ident16, mask_kq, mask_qk, gate_z, wide):
    LN_WRITES = 1 + NCOMP
    LINKS = 7
    NR = 8
    LINE = 4 * H * 4
    NLN = TT * 2 * H
    with ExitStack() as ctx:
        def sb(name, shape, dt=F32):
            return ctx.enter_context(nc.sbuf_tensor(name, shape, dt))

        def pb(name, shape):
            return ctx.enter_context(nc.psum_tensor(name, shape, F32))

        def sem(name):
            return ctx.enter_context(nc.semaphore(name))

        wqk = sb("wqk", [P, NK, 2 * D])
        wv = sb("wv", [P, NK, 2 * D])
        wl = sb("wl", [P, NK, LINE + H])
        bqk = sb("bqk", [P, 4])
        bqs = sb("bqs", [P, 4])
        bv = sb("bv", [P, 2 * D])
        bg = sb("bg", [P, H])
        incb = sb("incb", [P, H])
        xc = [sb(f"xc{i}", [P, NK, CH + 1]) for i in range(2)]
        vn = [sb(f"vn{i}", [P, 2 * H, VW]) for i in range(2)]
        gs = sb("gs", [P, 2, TT * 2, H * 4])
        gz = sb("gz", [P, TT, H])
        prod_a = sb("prod_a", [P, NLN, NCOMP])
        prod_b = sb("prod_b", [P, NLN, NCOMP])
        line = sb("line", [P, NLN, NCOMP])
        sq = sb("sq", [P, NLN, NCOMP])
        sum6 = sb("sum6", [P, NLN])
        ss = sb("ss", [P, NLN])
        nrm = sb("nrm", [P, NLN])
        rn = sb("rn", [P, TT, 2, H])
        rinc = sb("rinc", [P, TT, H])
        rneg = sb("rneg", [P, TT, H])
        most = sb("most", [P, 1])
        ln = sb("ln", [P, TT, 2, H, DH])
        t32 = [sb(f"t32_{i}", [P, CH]) for i in range(4)]
        d32 = [sb(f"d32_{i}", [P, CH]) for i in range(4)]
        sp3 = [sb(f"sp3_{i}", [P, NPART, CH], BF16) for i in range(NR)]
        pn = [pb(f"pn{i}", [P, 2, CH]) for i in range(2)]
        pr = [pb(f"pr{i}", [P, CH]) for i in range(4)]

        w_in = sem("w_in")
        x_in = [sem(f"x_in{i}") for i in range(2)]
        n_ready = sem("n_ready")
        v_out = sem("v_out")
        g_out = sem("g_out")
        v_st = [sem(f"v_st{i}") for i in range(2)]
        rows_ready = sem("rows_ready")
        row_act = sem("row_act")
        d_done = sem("d_done")
        p2_done = sem("p2_done")
        p3_done = sem("p3_done")
        s_st = [sem(f"s_st{i}") for i in range(NR)]
        ss_ready = sem("ss_ready")
        nrm_ready = sem("nrm_ready")
        ln_ready = sem("ln_ready")
        zero_ready = sem("zero_ready")
        id_ready = sem("id_ready")
        passed = sem("sp_passed1")
        wide_ready = sem("wide_ready")
        dve = sem("dve")
        block = ctx.enter_context(nc.Block())

        @block.sync
        def _(q):
            q.dma_start(xc[0][:, :, :], xt[0].rearrange("(k p) t -> p k t", p=P)).then_inc(x_in[0], 16)
            q.dma_start(wv[:, :, :], w_v.rearrange("(k p) n -> p k n", p=P)).then_inc(w_in, 16)
            q.dma_start(wl[:, :, :], w_line.rearrange("(k p) n -> p k n", p=P)).then_inc(w_in, 16)
            q.dma_start(wqk[:, :, :], w_qk.rearrange("(k p) n -> p k n", p=P)).then_inc(w_in, 16)
            q.dma_start(xc[1][:, :, :], xt[1].rearrange("(k p) t -> p k t", p=P)).then_inc(x_in[1], 16)

            def store_v(c, tt):
                q.wait_ge(v_out, c * TT + tt + 1)
                q.sem_inc(passed, 1)
                dst = values[:, :, :, :].rearrange("(a b g) p k n -> a b k p g n", a=2, b=B)
                for a in range(2):
                    q.dma_start(dst[ORDER[a], c // CPB, (c % CPB) * TT + tt, :, :, :],
                                vn[tt % 2][:, a * H:(a + 1) * H, :].rearrange("p (g h) w -> p g (h w)", g=NG))\
                     .then_inc(v_st[tt % 2], 16)

            def store_row(c, m):
                q.wait_ge(p3_done, c * NR + m + 1)
                q.sem_inc(passed, 1)
                q.dma_start(
                    parts[(m // 2) % 2, ORDER[m // 4], c // CPB, :, (m % 2) * P:(m % 2 + 1) * P,
                          bass.ds((c % CPB) * CH, CH)].rearrange("s r t -> r s t"),
                    sp3[m][:, :, :]).then_inc(s_st[m], 16)

            def load_x(c, par):
                q.wait_ge(rows_ready, (c - 2) * NR + 4)
                q.sem_inc(passed, 1)
                q.dma_start(xc[par][:, :, :], xt[c].rearrange("(k p) t -> p k t", p=P)).then_inc(x_in[par], 16)

            def stores(c):
                for tt in range(TT):
                    store_v(c, tt)
                    store_row(c - 1, tt)
                for m in range(4, NR):
                    store_row(c - 1, m)

            for tt in range(TT):
                store_v(0, tt)
            with q.Fori(0, NC // 2 - 1) as k:
                for par in range(2):
                    c = 2 * k + 1 + par
                    load_x(c + 1, par)
                    stores(c)
            stores(NC - 1)
            for m in range(NR):
                store_row(NC - 1, m)
            for i in range(2):
                q.wait_ge(v_st[i], NC * TT // 2 * 32)
            for m in range(NR):
                q.wait_ge(s_st[m], NC * 16)

        @block.gpsimd
        def _(g):
            g.memset(ident[:, :], 0.0).then_inc(id_ready, 1)
            g.memset(ident16[:, :], 0.0).then_inc(id_ready, 1)
            g.memset(mask_kq[:, :], 0.0).then_inc(id_ready, 1)
            g.memset(mask_qk[:, :], 0.0).then_inc(id_ready, 1)
            for i in range(2):
                g.memset(vn[i][:, :, :], 0.0).then_inc(id_ready, 1)
            g.memset(ln[:, :, :, :, :], 0.0).then_inc(id_ready, 1)
            g.wait_ge(id_ready, 7)
            for i in range(2):
                g.memset(vn[i][:, :, DH:DH + 1], 1.0).then_inc(zero_ready, 1)
            for m in (ident, ident16):
                g.affine_select(out=m[:, :], in_=m[:, :], compare_op=ALU.not_equal, fill=1.0, base=0,
                                pattern=[[-1, P]], channel_multiplier=1).then_inc(id_ready, 1)
            g.affine_select(out=mask_kq[:, :], in_=mask_kq[:, :], compare_op=ALU.is_ge, fill=MASKED,
                            base=0, pattern=[[1, P]], channel_multiplier=-1).then_inc(id_ready, 1)
            g.affine_select(out=mask_qk[:, :], in_=mask_qk[:, :], compare_op=ALU.is_ge, fill=MASKED,
                            base=0, pattern=[[-1, P]], channel_multiplier=1).then_inc(id_ready, 1)
            with g.Fori(0, NC) as c:
                for m in range(NR):
                    g.wait_ge(p2_done, c * NR + m + 1)
                    g.tensor_tensor(out=sp3[m][:, 2, :], in0=d32[m % 4][:, :],
                                    in1=sp3[m][:, 1, :], op=ALU.subtract).then_inc(p3_done, 1)

        @block.tensor
        def _(pe):
            pe.wait_ge(w_in, 7 * 16)
            pe.wait_ge(id_ready, 11)

            def token_tiles(c, par, loads, head):
                pe.wait_ge(x_in[par], loads * 16)
                for tt in range(TT):
                    if not (head and tt < 2):
                        pe.wait_ge(v_out, c * TT + tt - 1)
                        pe.wait_ge(g_out, (c * TT + tt - 1) * 2)
                    tok = slice(1 + tt * P, 1 + (tt + 1) * P)
                    prev = slice(tt * P, (tt + 1) * P)
                    bank = pn[tt % 2]
                    for k in range(NK):
                        pe.matmul(bank[:, 0, :], xc[par][:, k, tok], wv[:, k, :], start=k == 0, stop=k == NK - 1)
                    for k in range(NK):
                        pe.matmul(bank[:, 1, 0:H * 4], xc[par][:, k, prev], wl[:, k, 0:H * 4],
                                  start=k == 0, stop=k == NK - 1)
                    for k in range(NK):
                        last = pe.matmul(bank[:, 1, H * 4:LINE + H], xc[par][:, k, tok], wl[:, k, H * 4:],
                                         start=k == 0, stop=k == NK - 1)
                    last.then_inc(n_ready, 1)

            def qk_rows(c, par, head):
                for m in range(4):
                    if not head:
                        pe.wait_ge(row_act, (c * NR + m - 3) * 2)
                    for k in range(NK):
                        last = pe.matmul(pr[m][:, :], wqk[:, k, m * P:(m + 1) * P], xc[par][:, k, 1:],
                                         start=k == 0, stop=k == NK - 1)
                    last.then_inc(rows_ready, 1)

            def line_rows(c):
                pe.wait_ge(ln_ready, (c + 1) * LN_WRITES)
                for m in range(4, NR):
                    pe.wait_ge(row_act, (c * NR + m - 3) * 2)
                    for tt in range(TT):
                        src = ln[:, tt, (m - 4) // 2, (m % 2) * 8:(m % 2) * 8 + 8, :]
                        last = pe.transpose(pr[m % 4][:, tt * P:(tt + 1) * P],
                                            src.rearrange("p h d -> p (h d)"), ident[:, :])
                    last.then_inc(rows_ready, 1)

            token_tiles(0, 0, 1, True)
            qk_rows(0, 0, True)
            token_tiles(1, 1, 1, False)
            line_rows(0)
            qk_rows(1, 1, False)
            with pe.Fori(1, NC // 2) as k:
                for par in range(2):
                    c = 2 * k + par
                    token_tiles(c, par, k + 1, False)
                    line_rows(c - 1)
                    qk_rows(c, par, False)
            line_rows(NC - 1)

        @block.scalar
        def _(act):
            act.dma_start(bqk[:, :], b_qk).then_inc(w_in, 16)
            act.dma_start(bv[:, :], b_v.partition_broadcast(P)).then_inc(w_in, 16)
            act.dma_start(bg[:, :], b_gate.partition_broadcast(P)).then_inc(w_in, 16)
            act.dma_start(incb[:, :], inc.partition_broadcast(P)).then_inc(w_in, 16)
            act.wait_ge(dve, 2)

            def row_in(c, m, head):
                bias = bqs[:, m:m + 1] if m < 4 else 0.0
                scale = SCALE_Q if m < 2 else 1.0
                act.wait_ge(rows_ready, c * NR + m + 1)
                if not (head and m < 4):
                    act.wait_ge(d_done, c * NR + m - 3)
                if not head:
                    act.wait_ge(s_st[m], c * 16)
                act.activation(t32[m % 4][:, :], pr[m % 4][:, :], ACT.Identity, bias=bias, scale=scale)\
                   .then_inc(row_act, 1)
                act.activation(sp3[m][:, 0, :], pr[m % 4][:, :], ACT.Identity, bias=bias, scale=scale)\
                   .then_inc(row_act, 1)

            def second_part(c, m):
                act.wait_ge(d_done, c * NR + m + 1)
                act.activation(sp3[m][:, 1, :], d32[m % 4][:, :], ACT.Copy).then_inc(p2_done, 1)

            def points(c, tt, head):
                act.wait_ge(n_ready, c * TT + tt + 1)
                if tt == 0 and not head:
                    act.wait_ge(dve, (c - 1) * LINKS + 4)
                bank = pn[tt % 2][:, 1, :]
                act.activation(gs[:, :, 2 * tt:2 * tt + 2, :],
                               bank[:, 0:LINE].rearrange("p (y w n) -> p w y n", y=2, w=2),
                               ACT.Copy).then_inc(g_out, 1)
                act.activation(gz[:, tt, :], bank[:, LINE:LINE + H], ACT.Copy).then_inc(g_out, 1)

            def lengths(c):
                act.wait_ge(ss_ready, c + 1)
                act.activation(nrm[:, :], ss[:, :], ACT.Sqrt).then_inc(nrm_ready, 1)

            def line_rows(c, head):
                for m in range(4, NR):
                    row_in(c, m, head)
                    if m > 4:
                        second_part(c, m - 1)
                second_part(c, NR - 1)

            def chunk(c, head, second):
                for tt in range(TT):
                    points(c, tt, head)
                    if not head:
                        second_part(c - 1, tt)
                if not head:
                    line_rows(c - 1, second)
                for m in range(4):
                    row_in(c, m, head)
                lengths(c)

            chunk(0, True, False)
            chunk(1, False, True)
            with act.Fori(2, NC) as c:
                chunk(c, False, False)
            for m in range(4):
                second_part(NC - 1, m)
            line_rows(NC - 1, False)

        @block.vector
        def _(v):
            v.wait_ge(w_in, 7 * 16)
            v.tensor_scalar(bqs[:, 0:2], bqk[:, 0:2], SCALE_Q, None, ALU.mult).then_inc(dve, 1)
            v.tensor_copy(bqs[:, 2:4], bqk[:, 2:4]).then_inc(dve, 1)
            v.tensor_reduce(out=most[:, :], in_=incb[:, :], axis=AX.X, op=ALU.max,
                            apply_absolute_value=True).then_inc(dve, 1)
            v.wait_ge(dve, 3)
            v.tensor_scalar(wide[:, :], most[:, :], GEO_SAFE, None, ALU.is_gt).then_inc(wide_ready, 1)
            v.wait_ge(zero_ready, 2)
            v.wait_ge(id_ready, 11)
            p1, p2 = (gs[:, w, :, :].rearrange("p y (h c) -> p (y h) c", c=4) for w in range(2))
            line_v = line[:, :, :].rearrange("p (t y h) c -> p t y h c", t=TT, y=2)

            def first_rest(c, m, head):
                v.wait_ge(row_act, (c * NR + m + 1) * 2)
                if not (head and m < 4):
                    v.wait_ge(p3_done, c * NR + m - 3)
                v.tensor_tensor(out=d32[m % 4][:, :], in0=t32[m % 4][:, :], in1=sp3[m][:, 0, :],
                                op=ALU.subtract).then_inc(d_done, 1)

            def chunk(c, head, second):
                base = c * LINKS + 3
                for tt in range(TT):
                    v.wait_ge(n_ready, c * TT + tt + 1)
                    if not (head and tt < 2):
                        v.wait_ge(v_st[tt % 2], (c * (TT // 2) + tt // 2) * 32)
                    v.tensor_tensor(out=vn[tt % 2][:, :, 0:DH],
                                    in0=pn[tt % 2][:, 0, :].rearrange("p (h d) -> p h d", d=DH),
                                    in1=bv[:, :].rearrange("p (h d) -> p h d", d=DH),
                                    op=ALU.add).then_inc(v_out, 1)
                    if not head:
                        first_rest(c - 1, tt, second)
                if not head:
                    for m in range(4, NR):
                        first_rest(c - 1, m, second)
                v.wait_ge(g_out, (c + 1) * TT * 2)
                v.tensor_tensor(out=gate_z[:, bass.ds(c * TT, TT), :], in0=gz[:, :, :],
                                in1=bg[:, :].unsqueeze(1).to_broadcast([P, TT, H]), op=ALU.add)
                o = 0
                for i in range(3):
                    n = 3 - i
                    v.tensor_tensor(out=prod_a[:, :, o:o + n], in0=p1[:, :, i:i + 1].to_broadcast([P, NLN, n]),
                                    in1=p2[:, :, i + 1:4], op=ALU.mult)
                    last = v.tensor_tensor(out=prod_b[:, :, o:o + n], in0=p1[:, :, i + 1:4],
                                           in1=p2[:, :, i:i + 1].to_broadcast([P, NLN, n]), op=ALU.mult)
                    o += n
                last.then_inc(dve, 1)
                v.wait_ge(dve, base + 1)
                v.tensor_tensor(out=line[:, :, :], in0=prod_a[:, :, :], in1=prod_b[:, :, :],
                                op=ALU.subtract).then_inc(dve, 1)
                v.wait_ge(dve, base + 2)
                v.tensor_tensor(out=sq[:, :, :], in0=line[:, :, :], in1=line[:, :, :], op=ALU.mult)\
                 .then_inc(dve, 1)
                v.wait_ge(dve, base + 3)
                v.tensor_reduce(out=sum6[:, :], in_=sq[:, :, :], axis=AX.X, op=ALU.add).then_inc(dve, 1)
                v.wait_ge(dve, base + 4)
                if not head:
                    v.wait_ge(nrm_ready, c)
                v.tensor_scalar(ss[:, :], sum6[:, :], 1e-24, None, ALU.max).then_inc(ss_ready, 1)
                v.wait_ge(nrm_ready, c + 1)
                v.reciprocal(rn[:, :, :, :].rearrange("p t y h -> p (t y h)"), nrm[:, :]).then_inc(dve, 1)
                v.wait_ge(dve, base + 5)
                v.tensor_tensor(out=rinc[:, :, :], in0=rn[:, :, 1, :],
                                in1=incb[:, :].unsqueeze(1).to_broadcast([P, TT, H]), op=ALU.mult)\
                 .then_inc(dve, 1)
                v.wait_ge(dve, base + 6)
                v.tensor_scalar(rneg[:, :, :], rinc[:, :, :], -1.0, None, ALU.mult).then_inc(dve, 1)
                v.wait_ge(dve, base + 7)
                if not head:
                    v.wait_ge(rows_ready, c * NR)
                v.tensor_tensor(
                    out=ln[:, :, 1, :, 0:NCOMP], in0=line_v[:, :, 0, :, :],
                    in1=rn[:, :, 0, :].unsqueeze(3).to_broadcast([P, TT, H, NCOMP]),
                    op=ALU.mult).then_inc(ln_ready, 1)
                for i in range(NCOMP):
                    v.tensor_tensor(out=ln[:, :, 0, :, NCOMP - 1 - i], in0=line_v[:, :, 1, :, i],
                                    in1=(rinc if J_SIGN[i] > 0 else rneg)[:, :, :],
                                    op=ALU.mult).then_inc(ln_ready, 1)

            chunk(0, True, False)
            chunk(1, False, True)
            with v.Fori(2, NC) as c:
                chunk(c, False, False)
            for m in range(NR):
                first_rest(NC - 1, m, False)


def attend(nc, parts, values, heads, ident, ident16, mask_kq, mask_qk, wide):
    with ExitStack() as ctx:
        def sb(name, shape, dt=F32):
            return ctx.enter_context(nc.sbuf_tensor(name, shape, dt))

        def pb(name, shape):
            return ctx.enter_context(nc.psum_tensor(name, shape, F32))

        def sem(name):
            return ctx.enter_context(nc.semaphore(name))

        qa = [sb(f"qa{i}", [P, HG, T], BF16) for i in range(2)]
        ka = [sb(f"ka{i}", [P, HG, T], BF16) for i in range(2)]
        va = [sb(f"va{i}", [P, NKB, HG * VW]) for i in range(2)]
        prob = [sb(f"prob{i}", [P, 2 * CH]) for i in range(8)]
        ot = [sb(f"ot{i}", [P, CH]) for i in range(2)]
        rz = sb("rz", [P, TT * HG])
        on = [sb(f"on{i}", [P, TT, HG * DH]) for i in range(2)]
        mp = [sb(f"mp{i}", [P, HG * NKB, NKB * P // CH]) for i in range(2)]
        negm = sb("negm", [P, P])
        mrow = sb("mrow", [HG * NKB, 2, P], BF16)
        ex = pb("ex", [P, 2, 2 * CH])
        mx = pb("mx", [P, 2, CH])
        pv = pb("pv", [P, 2, CH])

        qk_in = [[sem(f"qk_in{i}_{j}") for j in range(2)] for i in range(2)]
        v_in = [sem(f"v_in{i}") for i in range(2)]
        m_in = sem("m_in")
        ones_ready = sem("ones_ready")
        ex_ready = sem("ex_ready")
        ex_done = sem("ex_done")
        pv_step = sem("pv_step")
        ot_ready = sem("ot_ready")
        tr_done = sem("tr_done")
        rz_ready = sem("rz_ready")
        on_ready = sem("on_ready")
        on_st = [sem(f"on_st{i}") for i in range(2)]
        mx_ready = [sem(f"mx_ready{i}") for i in range(2)]
        mx_free = [sem(f"mx_free{i}") for i in range(2)]
        negm_ready = [sem(f"negm_ready{i}") for i in range(2)]
        m_hi = [sem(f"m_hi{i}") for i in range(2)]
        mrow_ready = sem("mrow_ready")
        passed = sem("sp_passed2")
        block = ctx.enter_context(nc.Block())

        @block.sync
        def _(q):
            def load_qk(it, par):
                a, b, g = it // (B * NG), (it // NG) % B, it % NG
                for j in range(2):
                    for side, dst, order in ((0, qa, Q_PARTS), (1, ka, K_PARTS)):
                        for n, s in enumerate(order):
                            src = parts[side, a, b, s, bass.ds(g * (HG * DH) + j * 2 * DH, 2 * DH), :]
                            q.dma_start(dst[par][n * DH:(n + 1) * DH, 2 * j:2 * j + 2, :],
                                        src.rearrange("(h d) t -> d h t", h=2)).then_inc(qk_in[par][j], 16)

            def load_v(it, par):
                q.dma_start(va[par][:, :, :], values[it]).then_inc(v_in[par], 16)

            def store(it, qt):
                q.wait_ge(on_ready, it * NQT + qt + 1)
                q.sem_inc(passed, 1)
                q.dma_start(heads[it, :, qt * TT:(qt + 1) * TT, :],
                            on[qt % 2][:, :, :]).then_inc(on_st[qt % 2], 16)

            def rows(it, par):
                q.wait_ge(mrow_ready, it + 1)
                q.sem_inc(passed, 1)
                for i in range(2):
                    q.dma_start(qa[par][NROW + i:NROW + i + 1, :, :].rearrange("p h (k t) -> p (h k) t", t=P),
                                mrow[:, i, :]).then_inc(m_in, 16)

            def item(it, par, has_prev, has_next):
                if has_next:
                    if has_prev:
                        q.wait_ge(ex_ready, it * NEX)
                        q.sem_inc(passed, 1)
                    load_qk(it + 1, 1 - par)
                if has_prev:
                    store(it - 1, NQT - 1)
                if has_next:
                    if has_prev:
                        q.wait_ge(pv_step, it * NSTEP)
                        q.sem_inc(passed, 1)
                    load_v(it + 1, 1 - par)
                for qt in range(NQT - 1):
                    store(it, qt)
                if has_next:
                    rows(it + 1, 1 - par)

            load_qk(0, 0)
            load_v(0, 0)
            rows(0, 0)
            item(0, 0, False, True)
            with q.Fori(0, ITEMS // 2 - 1) as k:
                item(2 * k + 1, 1, True, True)
                item(2 * k + 2, 0, True, True)
            item(ITEMS - 1, 1, True, False)
            store(ITEMS - 1, NQT - 1)
            for i in range(2):
                q.wait_ge(on_st[i], ITEMS * NQT // 2 * 16)

        @block.gpsimd
        def _(g):
            g.memset(negm[:, :], 0.0).then_inc(ones_ready, 1)
            for i in range(2):
                g.wait_ge(ones_ready, 2 * i + 1)
                g.memset(ka[i][NROW:NROWM, :, :], 1.0).then_inc(ones_ready, 1)
                g.wait_ge(ones_ready, 2 * i + 2)
                g.memset(mp[i][:, :, :], MASKED).then_inc(ones_ready, 1)

        @block.tensor
        def _(pe):
            pe.wait_ge(ones_ready, 5)
            is_wide = pe.value_load(wide[0:1, 0:1], min_val=0, max_val=1)

            def scores(it, par, s, h, head):
                n = s * HG + h
                slot = n % 2
                if not (head and n < 2):
                    pe.wait_ge(ex_done, it * NEX + n - 1)
                qt, blocks = STEPS[s]
                at, _ = place(s)
                for (kb, w), c0 in zip(blocks, at):
                    dst = ex[:, slot, c0:c0 + w]
                    on_diagonal = kb >= TT * qt
                    last = pe.matmul(dst, ka[par][0:NROWM, h, kb * P:(kb + 1) * P],
                                     qa[par][0:NROWM, h, (qt + 1) * CH - w:(qt + 1) * CH],
                                     start=True, stop=not on_diagonal)
                    if on_diagonal:
                        last = pe.matmul(dst[:, 0:P], ident16[:, :], mask_kq[:, :], start=False, stop=True)
                last.then_inc(ex_ready, 1)

            def max_tile(it, par, use, a, u):
                kind, at = a
                h, qb, k0, w, on_diagonal = MAXT[u]
                slot = (par + u) % 2
                if u == 0:
                    pe.wait_ge(mrow_ready, it)
                if qb == 0 and h % 2 == 0:
                    pe.wait_ge(qk_in[par][h // 2], use * 12 * 16)
                if u >= 2:
                    pe.wait_ge(mx_free[kind], at * NMT + u - 1)
                dst = mx[:, slot, 0:w]
                last = pe.matmul(dst, qa[par][0:NROW, h, qb * P:(qb + 1) * P],
                                 ka[par][0:NROW, h, k0:k0 + w], start=True, stop=not on_diagonal)
                if on_diagonal:
                    last = pe.matmul(dst[:, w - P:w], ident16[:, :], mask_qk[:, :], start=False, stop=True)
                last.then_inc(mx_ready[kind], 1)

            def max_rows(par, a):
                kind, at = a
                pe.wait_ge(negm_ready[kind], at + 1)
                pe.transpose(mx[:, par, 0:P], negm[:, :], ident[:, :]).then_inc(mx_ready[kind], 1)

            def wide_maxima(it, par, use):
                with pe.If(is_wide > 0):
                    for u in range(NMT):
                        max_tile(it, par, use, (GEO, it), u)
                    max_rows(par, (GEO, it))

            def times_v(it, par, s, j, head):
                qt, blocks = STEPS[s]
                kb, w = blocks[j]
                at, _ = place(s)
                if j == 0:
                    pe.wait_ge(ex_done, it * NEX + s * HG + HG)
                    if s == 0:
                        pe.wait_ge(v_in[par], (it // 2 + 1) * 16)
                    if s == FIRST_OF[qt] and not (head and qt < 2):
                        pe.wait_ge(on_ready, it * NQT + qt - 1)
                end = j == 1 and s == LAST_OF[qt]
                for h in range(HG):
                    last = pe.matmul(pv[h * VW:(h + 1) * VW, qt % 2, CH - w:CH],
                                     va[par][:, kb, h * VW:(h + 1) * VW],
                                     prob[(s * HG + h) % 8][:, at[j]:at[j] + w],
                                     start=kb == 0, stop=end, tile_position=(0, h * VW))
                if j == 1:
                    last.then_inc(pv_step, 1)

            def turn(it, qt):
                pe.wait_ge(ot_ready, it * NQT + qt + 1)
                for i in range(TT):
                    last = pe.transpose(pv[:, qt % 2, i * P:(i + 1) * P], ot[qt % 2][:, i * P:(i + 1) * P],
                                        ident[:, :])
                last.then_inc(tr_done, 1)

            def step(it, par, s, head, nxt):
                later = list(SPREAD[s]) if nxt == DOT else []
                each = -(-len(later) // 6)

                def some(n):
                    for _ in range(min(n, len(later))):
                        max_tile(it + 1, 1 - par, NEXT_USE(it, par), (DOT, it + 1 - ITEMS // 2), later.pop(0))

                before = (it, par, s - 1) if s else (it - 1, 1 - par, NSTEP - 1)
                has_before = not (head and s == 0)
                scores(it, par, s, 0, head)
                some(each)
                scores(it, par, s, 1, head)
                some(each)
                if has_before:
                    times_v(*before, 0, head)
                some(2 * each)
                scores(it, par, s, 2, head)
                some(each)
                scores(it, par, s, 3, head)
                some(each)
                if has_before:
                    times_v(*before, 1, head)
                some(NMT)
                if s == MT_STEP:
                    if nxt == DOT:
                        max_rows(1 - par, (DOT, it + 1 - ITEMS // 2))
                    elif nxt == GEO:
                        wide_maxima(it + 1, 1 - par, NEXT_USE(it, par))
                for qt in range(NQT):
                    if s - 2 == LAST_OF[qt]:
                        turn(it, qt)
                if s == 1 and not head:
                    turn(it - 1, NQT - 1)

            def NEXT_USE(it, par):
                return (it + 1) // 2 + 1

            def item(it, par, head, nxt):
                for j in range(2):
                    pe.wait_ge(qk_in[par][j], (it // 2 + 1) * 12 * 16)
                pe.wait_ge(m_in, (it + 1) * 32)
                for s in range(NSTEP):
                    step(it, par, s, head, nxt)

            wide_maxima(0, 0, 1)
            item(0, 0, True, GEO)
            with pe.Fori(0, ITEMS // 4 - 1) as k:
                item(2 * k + 1, 1, False, GEO)
                item(2 * k + 2, 0, False, GEO)
            with pe.Fori(ITEMS // 4 - 1, ITEMS // 2 - 1) as k:
                item(2 * k + 1, 1, False, DOT)
                item(2 * k + 2, 0, False, DOT)
            item(ITEMS - 1, 1, False, None)
            for j in range(2):
                times_v(ITEMS - 1, 1, NSTEP - 1, j, False)
            turn(ITEMS - 1, NQT - 1)

        @block.scalar
        def _(act):
            def item(it, head):
                for n in range(NEX):
                    s = n // HG
                    _, w = place(s)
                    act.wait_ge(ex_ready, it * NEX + n + 1)
                    if n % HG == 0 and not (head and s < 2):
                        act.wait_ge(pv_step, it * NSTEP + s - 1)
                    act.activation(prob[n % 8][:, 0:w], ex[:, n % 2, 0:w], ACT.Exp).then_inc(ex_done, 1)

            item(0, True)
            with act.Fori(1, ITEMS) as it:
                item(it, False)

        @block.vector
        def _(v):
            v.wait_ge(ones_ready, 5)
            is_wide = v.value_load(wide[0:1, 0:1], min_val=0, max_val=1)

            def max_tile(par, a, u):
                kind, at = a
                h, qb, k0, w, _ = MAXT[u]
                v.wait_ge(mx_ready[kind], at * NMX + u + 1)
                v.tensor_reduce(out=mp[par][:, h * NKB + qb, k0 // CH:k0 // CH + 1], in_=mx[:, (par + u) % 2, 0:w],
                                axis=AX.X, op=ALU.max).then_inc(mx_free[kind], 1)

            def rows_free(it, first):
                if not first:
                    v.wait_ge(m_in, it * 32)

            def max_rows(it, par, a, first):
                kind, at = a
                v.wait_ge(mx_free[kind], (at + 1) * NMT)
                v.tensor_reduce(out=negm[:, 0:HG * NKB], in_=mp[par][:, :, :], axis=AX.X, op=ALU.max,
                                negate=True).then_inc(negm_ready[kind], 1)
                v.wait_ge(mx_ready[kind], (at + 1) * NMX)
                rows_free(it, first)
                src = mx[0:HG * NKB, par, 0:P]
                v.tensor_copy(mrow[:, 0, :], src).then_inc(m_hi[kind], 1)
                v.wait_ge(m_hi[kind], at + 1)
                v.tensor_tensor(out=mrow[:, 1, :], in0=src, in1=mrow[:, 0, :], op=ALU.subtract)\
                 .then_inc(mrow_ready, 1)

            def geo_rows(it, par, first):
                with v.If(is_wide > 0):
                    for u in range(NMT):
                        max_tile(par, (GEO, it), u)
                    max_rows(it, par, (GEO, it), first)
                with v.If(is_wide == 0):
                    rows_free(it, first)
                    v.memset(mrow[:, :, :], 0.0).then_inc(mrow_ready, 1)

            def take(it, qt, head):
                v.wait_ge(pv_step, it * NSTEP + LAST_OF[qt] + 1)
                if not (head and qt < 2):
                    v.wait_ge(tr_done, it * NQT + qt - 1)
                v.tensor_copy(ot[qt % 2][:, :], pv[:, qt % 2, :]).then_inc(ot_ready, 1)

            def normalise(it, qt, head):
                v.wait_ge(tr_done, it * NQT + qt + 1)
                if not (head and qt < 2):
                    v.wait_ge(on_st[qt % 2], (it * (NQT // 2) + qt // 2) * 16)
                src = pv[:, qt % 2, :].rearrange("p (n w) -> p n w", w=VW)
                v.reciprocal(rz[:, :].unsqueeze(2), src[:, :, DH:DH + 1]).then_inc(rz_ready, 1)
                v.wait_ge(rz_ready, it * NQT + qt + 1)
                v.tensor_tensor(out=on[qt % 2][:, :, :].rearrange("p s (h d) -> p (s h) d", d=DH),
                                in0=src[:, :, 0:DH], in1=rz[:, :].unsqueeze(2).to_broadcast([P, TT * HG, DH]),
                                op=ALU.mult).then_inc(on_ready, 1)

            def item(it, par, head, nxt):
                for s in range(NSTEP):
                    if nxt == DOT:
                        for u in SPREAD[s]:
                            max_tile(1 - par, (DOT, it + 1 - ITEMS // 2), u)
                    if s == MT_STEP:
                        if nxt == DOT:
                            max_rows(it + 1, 1 - par, (DOT, it + 1 - ITEMS // 2), False)
                        elif nxt == GEO:
                            geo_rows(it + 1, 1 - par, False)
                    if s == 0 and not head:
                        take(it - 1, NQT - 1, False)
                    if s == 1 and not head:
                        normalise(it - 1, NQT - 1, False)
                    for qt in range(NQT):
                        if s - 1 == LAST_OF[qt]:
                            take(it, qt, head)
                        if s - 2 == LAST_OF[qt]:
                            normalise(it, qt, head)

            geo_rows(0, 0, True)
            item(0, 0, True, GEO)
            with v.Fori(0, ITEMS // 4 - 1) as k:
                item(2 * k + 1, 1, False, GEO)
                item(2 * k + 2, 0, False, GEO)
            with v.Fori(ITEMS // 4 - 1, ITEMS // 2 - 1) as k:
                item(2 * k + 1, 1, False, DOT)
                item(2 * k + 2, 0, False, DOT)
            item(ITEMS - 1, 1, False, None)
            take(ITEMS - 1, NQT - 1, False)
            normalise(ITEMS - 1, NQT - 1, False)


def finish(nc, x, heads, gate_z, ident, out_w, out_b, wg, wu, wd, out):
    NT = NC * TT
    NM = HID // P
    with ExitStack() as ctx:
        def sb(name, shape, dt=F32):
            return ctx.enter_context(nc.sbuf_tensor(name, shape, dt))

        def pb(name, shape):
            return ctx.enter_context(nc.psum_tensor(name, shape, F32))

        def sem(name):
            return ctx.enter_context(nc.semaphore(name))

        wo = sb("wo", [P, NK, D])
        ob = sb("ob", [P, D])
        wgi = sb("wgi", [P, NK, HID], I32)
        wui = sb("wui", [P, NK, HID], I32)
        wdi = sb("wdi", [P, NM, D], I32)
        wgf = sb("wgf", [P, NK, HID])
        wuf = sb("wuf", [P, NK, HID])
        wdf = sb("wdf", [P, NM, D])
        ez = sb("ez", [P, NT, H])
        gsum = sb("gsum", [P, NT])
        gate = sb("gate", [P, NT])
        omg = sb("omg", [P, NT])
        att = [[sb(f"att{a}_{i}", [P, TT, D]) for i in range(2)] for a in range(2)]
        xin = [sb(f"xin{i}", [P, TT, D]) for i in range(2)]
        mix = [sb(f"mix{i}", [P, TT, D]) for i in range(2)]
        ct = [sb(f"ct{i}", [P, NK, CH]) for i in range(2)]
        res = sb("res", [P, NT, D])
        rch = [sb(f"rch{i}", [P, TT, D]) for i in range(2)]
        stat = sb("stat", [P, TT, 6])
        mvc = sb("mvc", [P, TT, 2])
        mv = sb("mv", [P, NT, 2])
        std = sb("std", [P, NT])
        rstd = sb("rstd", [P, NT])
        sg = [sb(f"sg{i}", [P, CH]) for i in range(2)]
        ht = [sb(f"ht{i}", [P, NM, CH]) for i in range(2)]
        pt = pb("pt", [P, NK, CH])
        pg = [pb(f"pg{i}", [P, 2, CH]) for i in range(2)]
        po = [pb(f"po{i}", [P, CH]) for i in range(2)]

        w_in = sem("w_in3")
        att_in = [sem(f"att_in{i}") for i in range(2)]
        wf_ready = sem("wf_ready")
        e_ready = sem("e_ready")
        dve = sem("dve3")
        gate_ready = sem("gate_ready")
        xb_ready = sem("xb_ready")
        mix_tmp = sem("mix_tmp")
        mix_ready = sem("mix_ready")
        pt_ready = sem("pt_ready")
        ct_ready = sem("ct_ready")
        po_ready = sem("po_ready")
        res_ready = sem("res_ready")
        kept = sem("kept")
        st_ready = sem("st_ready")
        mvc_ready = sem("mvc_ready")
        mv_ready = sem("mv_ready")
        std_ready = sem("std_ready")
        rstd_ready = sem("rstd_ready")
        y_ready = sem("y_ready")
        pg_ready = sem("pg_ready")
        sg_ready = sem("sg_ready")
        ht_ready = sem("ht_ready")
        o_ready = sem("o_ready")
        o_st = sem("o_st")
        passed = sem("sp_passed3")
        v_passed = sem("v_passed")
        block = ctx.enter_context(nc.Block())

        x_v = x.rearrange("(c t p) n -> c p t n", p=P, t=TT)
        out_v = out.rearrange("(c t p) n -> c p t n", p=P, t=TT)
        heads_v = heads[:, :, :, :].rearrange("(a b g) p k n -> a b g p k n", a=2, b=B)

        @block.sync
        def _(q):
            q.dma_start(wo[:, :, :], out_w.rearrange("(k p) n -> p k n", p=P)).then_inc(w_in, 16)
            q.dma_start(ob[:, :], out_b.partition_broadcast(P)).then_inc(w_in, 16)
            q.dma_start(wgi[:, :, :], wg.rearrange("(k p) n -> p k n", p=P)).then_inc(w_in, 16)
            q.dma_start(wui[:, :, :], wu.rearrange("(k p) n -> p k n", p=P)).then_inc(w_in, 16)
            q.dma_start(wdi[:, :, :], wd.rearrange("(k p) n -> p k n", p=P)).then_inc(w_in, 16)

            def load(c, par):
                for a in range(2):
                    for g in range(NG):
                        q.dma_start(att[a][par][:, :, g * HG * DH:(g + 1) * HG * DH],
                                    heads_v[a, c // CPB, g, :, bass.ds((c % CPB) * TT, TT), :])\
                         .then_inc(att_in[par], 16)
                q.dma_start(xin[par][:, :, :], x_v[c]).then_inc(att_in[par], 16)

            load(0, 0)
            load(1, 1)
            with q.Fori(1, NC // 2) as k:
                for par in range(2):
                    q.wait_ge(res_ready, (2 * k + par - 1) * TT)
                    q.sem_inc(passed, 1)
                    load(2 * k + par, par)
            with q.Fori(0, NC) as c:
                q.wait_ge(o_ready, (c + 1) * TT)
                q.sem_inc(passed, 1)
                q.dma_start(out_v[c], res[:, bass.ds(c * TT, TT), :]).then_inc(o_st, 16)
            q.wait_ge(o_st, NC * 16)

        @block.gpsimd
        def _(g):
            def keep(c, par, base):
                g.wait_ge(res_ready, (base + c + 1) * TT)
                g.tensor_copy(res[:, bass.ds(c * TT, TT), :], rch[par][:, :, :]).then_inc(kept, 1)

            g.wait_ge(w_in, 5 * 16)
            with g.Fori(0, NC // 2) as k:
                for par in range(2):
                    g.wait_ge(att_in[par], (k + 1) * 9 * 16)
                    g.tensor_tensor(out=xin[par][:, :, :], in0=xin[par][:, :, :],
                                    in1=ob[:, :].unsqueeze(1).to_broadcast([P, TT, D]), op=ALU.add)\
                     .then_inc(xb_ready, 1)
                    keep(2 * k + par, par, 0)
            with g.Fori(0, NC // 2) as k:
                for par in range(2):
                    keep(2 * k + par, par, NC)

        @block.tensor
        def _(pe):
            pe.wait_ge(w_in, 5 * 16)

            def transposes(src):
                for k in range(NK):
                    for tt in range(TT):
                        last = pe.transpose(pt[:, k, tt * P:(tt + 1) * P], src(tt, k), ident[:, :])
                last.then_inc(pt_ready, 1)

            def turn_mixed(c, par, head):
                pe.wait_ge(mix_ready, (c + 1) * TT)
                if not head:
                    pe.wait_ge(ct_ready, c)
                transposes(lambda tt, k: mix[par][:, tt, k * P:(k + 1) * P])

            def out_chunk(c, par, head):
                pe.wait_ge(ct_ready, c + 1)
                for tt in range(TT):
                    if not (head and tt < 2):
                        pe.wait_ge(res_ready, c * TT + tt - 1)
                    for k in range(NK):
                        last = pe.matmul(po[tt % 2][:, 0:D], ct[par][:, k, tt * P:(tt + 1) * P], wo[:, k, :],
                                         start=k == 0, stop=k == NK - 1)
                    last.then_inc(po_ready, 1)

            turn_mixed(0, 0, True)
            for c in range(2):
                turn_mixed(c + 1, 1 - c, False)
                out_chunk(c, c, c == 0)
            with pe.Fori(1, NC // 2 - 1) as k:
                for par in range(2):
                    turn_mixed(2 * k + par + 1, 1 - par, False)
                    out_chunk(2 * k + par, par, False)
            turn_mixed(NC - 1, 1, False)
            out_chunk(NC - 2, 0, False)
            out_chunk(NC - 1, 1, False)

            def turn_normed(c, par):
                pe.wait_ge(y_ready, (c + 1) * TT)
                pe.wait_ge(ct_ready, NC + c)
                transposes(lambda tt, k: mix[par][:, tt, k * P:(k + 1) * P])

            def hidden(c, par, head):
                pe.wait_ge(ct_ready, NC + c + 1)
                for m in range(NM):
                    if not (head and m < 2):
                        pe.wait_ge(ht_ready, c * NM + m - 1)
                    for i, w in enumerate((wgf, wuf)):
                        for k in range(NK):
                            last = pe.matmul(pg[m % 2][:, i, :], w[:, k, m * P:(m + 1) * P], ct[par][:, k, :],
                                             start=k == 0, stop=k == NK - 1)
                    last.then_inc(pg_ready, 1)

            def down(c, par):
                pe.wait_ge(ht_ready, (c + 1) * NM)
                for tt in range(TT):
                    pe.wait_ge(res_ready, NT + c * TT + tt - 1)
                    for m in range(NM):
                        last = pe.matmul(po[tt % 2][:, 0:D], ht[par][:, m, tt * P:(tt + 1) * P], wdf[:, m, :],
                                         start=m == 0, stop=m == NM - 1)
                    last.then_inc(po_ready, 1)

            turn_normed(0, 0)
            pe.wait_ge(wf_ready, 3)
            for c in range(2):
                hidden(c, c, c == 0)
                turn_normed(c + 1, 1 - c)
                down(c, c)
            with pe.Fori(1, NC // 2 - 1) as k:
                for par in range(2):
                    hidden(2 * k + par, par, False)
                    turn_normed(2 * k + par + 1, 1 - par)
                    down(2 * k + par, par)
            hidden(NC - 2, 0, False)
            turn_normed(NC - 1, 1)
            down(NC - 2, 0)
            hidden(NC - 1, 1, False)
            down(NC - 1, 1)

        @block.scalar
        def _(act):
            act.activation(ez[:, :, :], gate_z[:, :, :], ACT.Exp, scale=-1.0).then_inc(e_ready, 1)

            def columns(c, par, base, head):
                act.wait_ge(pt_ready, base + c + 1)
                if not head:
                    act.wait_ge(po_ready, (base + c - 1) * TT)
                act.activation(ct[par][:, :, :], pt[:, :, :], ACT.Copy).then_inc(ct_ready, 1)

            columns(0, 0, 0, True)
            columns(1, 1, 0, True)
            with act.Fori(1, NC // 2) as k:
                for par in range(2):
                    columns(2 * k + par, par, 0, False)

            def root(n):
                act.wait_ge(mv_ready, n * (NC + 1))
                act.activation(std[:, :], mv[:, :, 1], ACT.Sqrt).then_inc(std_ready, 1)

            root(1)

            def gates(c, head):
                for m in range(NM):
                    act.wait_ge(pg_ready, c * NM + m + 1)
                    if not (head and m < 2):
                        act.wait_ge(ht_ready, c * NM + m - 1)
                    act.activation(sg[m % 2][:, :], pg[m % 2][:, 0, :], ACT.Silu, scale=SCALE_W)\
                       .then_inc(sg_ready, 1)

            columns(0, 0, NC, False)
            for c in range(2):
                gates(c, c == 0)
                columns(c + 1, 1 - c, NC, False)
            with act.Fori(1, NC // 2 - 1) as k:
                for par in range(2):
                    gates(2 * k + par, False)
                    columns(2 * k + par + 1, 1 - par, NC, False)
            gates(NC - 2, False)
            columns(NC - 1, 1, NC, False)
            gates(NC - 1, False)
            root(2)

        @block.vector
        def _(v):
            v.wait_ge(e_ready, 1)
            v.tensor_scalar(ez[:, :, :], ez[:, :, :], 1.0, None, ALU.add).then_inc(dve, 1)
            v.wait_ge(dve, 1)
            v.reciprocal(ez[:, :, :], ez[:, :, :]).then_inc(dve, 1)
            v.wait_ge(dve, 2)
            v.tensor_reduce(out=gsum[:, :], in_=ez[:, :, :], axis=AX.X, op=ALU.add).then_inc(dve, 1)
            v.wait_ge(dve, 3)
            v.tensor_scalar(gate[:, :], gsum[:, :], 1.0 / H, None, ALU.mult).then_inc(gate_ready, 1)
            v.tensor_scalar(omg[:, :], gsum[:, :], -1.0 / H, 1.0, ALU.mult, ALU.add).then_inc(gate_ready, 1)
            v.wait_ge(gate_ready, 2)

            def mixed(c, par, head):
                v.wait_ge(att_in[par], (c // 2 + 1) * 9 * 16)
                if not head:
                    v.wait_ge(pt_ready, c - 1)
                for tt in range(TT):
                    n = c * TT + tt
                    v.tensor_scalar(mix[par][:, tt, :], att[DOT][par][:, tt, :], omg[:, bass.ds(n, 1)], None,
                                    ALU.mult).then_inc(mix_tmp, 1)
                v.wait_ge(mix_tmp, (c + 1) * TT)
                for tt in range(TT):
                    n = c * TT + tt
                    v.scalar_tensor_tensor(out=mix[par][:, tt, :], in0=att[GEO][par][:, tt, :],
                                           scalar=gate[:, bass.ds(n, 1)], in1=mix[par][:, tt, :],
                                           op0=ALU.mult, op1=ALU.add).then_inc(mix_ready, 1)

            def residual(c, par, base, head, scale):
                if not head:
                    v.wait_ge(kept, base // TT + c - 1)
                for tt in range(TT):
                    v.wait_ge(po_ready, base + c * TT + tt + 1)
                    if scale is None:
                        if tt == 0:
                            v.wait_ge(xb_ready, c + 1)
                        v.tensor_tensor(out=rch[par][:, tt, :], in0=po[tt % 2][:, 0:D], in1=xin[par][:, tt, :],
                                        op=ALU.add).then_inc(res_ready, 1)
                    else:
                        v.scalar_tensor_tensor(out=rch[par][:, tt, :], in0=po[tt % 2][:, 0:D], scalar=scale,
                                               in1=mix[par][:, tt, :], op0=ALU.mult, op1=ALU.add)\
                         .then_inc(res_ready, 1)
                v.wait_ge(res_ready, base + (c + 1) * TT)
                for tt in range(TT):
                    v.bn_stats(stat[:, tt, :], rch[par][:, tt, :]).then_inc(st_ready, 1)
                v.wait_ge(st_ready, base + (c + 1) * TT)
                v.sem_inc(v_passed, 1)
                for tt in range(TT):
                    last = v.bn_aggr(mvc[:, tt, :], stat[:, tt, :])
                last.then_inc(mvc_ready, 1)
                v.wait_ge(mvc_ready, base // TT + c + 1)
                v.tensor_copy(mv[:, bass.ds(c * TT, TT), :], mvc[:, :, :]).then_inc(mv_ready, 1)

            mixed(0, 0, True)
            mixed(1, 1, True)
            for c in range(2):
                residual(c, c, 0, True, None)
                mixed(c + 2, c, False)
            with v.Fori(1, NC // 2 - 1) as k:
                for par in range(2):
                    residual(2 * k + par, par, 0, False, None)
                    mixed(2 * k + par + 2, par, False)
            for c in (NC - 2, NC - 1):
                residual(c, c % 2, 0, False, None)

            def scales(n):
                v.wait_ge(mv_ready, n * (NC + 1) - 1)
                v.tensor_scalar(mv[:, :, 1], mv[:, :, 1], EPS, None, ALU.add).then_inc(mv_ready, 1)
                v.wait_ge(std_ready, n)
                v.reciprocal(rstd[:, :], std[:, :]).then_inc(rstd_ready, 1)
                v.wait_ge(rstd_ready, n)

            def norm(c, dst, done, base):
                v.wait_ge(kept, base + c + 1)
                for tt in range(TT):
                    n = c * TT + tt
                    v.tensor_scalar(dst(tt, n), res[:, bass.ds(n, 1), :].rearrange("p a n -> p (a n)"),
                                    mv[:, bass.ds(n, 1), 0:1].rearrange("p a n -> p (a n)"),
                                    rstd[:, bass.ds(n, 1)], ALU.subtract, ALU.mult).then_inc(done, 1)

            scales(1)
            v.wait_ge(w_in, 5 * 16)
            for wf, wi in ((wgf, wgi), (wuf, wui), (wdf, wdi)):
                v.tensor_copy(wf[:, :, :], wi[:, :, :]).then_inc(wf_ready, 1)

            def ffn_norm(c, par):
                norm(c, lambda tt, n: mix[par][:, tt, :], y_ready, 0)

            def ffn_chunk(c, par):
                for m in range(NM):
                    v.wait_ge(sg_ready, c * NM + m + 1)
                    v.scalar_tensor_tensor(out=ht[par][:, m, :], in0=pg[m % 2][:, 1, :], scalar=SCALE_W,
                                           in1=sg[m % 2][:, :], op0=ALU.mult, op1=ALU.mult).then_inc(ht_ready, 1)
                residual(c, par, NT, False, SCALE_W)

            ffn_norm(0, 0)
            ffn_norm(1, 1)
            with v.Fori(0, NC // 2 - 1) as k:
                for par in range(2):
                    c = 2 * k + par
                    ffn_chunk(c, par)
                    ffn_norm(c + 2, par)
            for c in (NC - 2, NC - 1):
                ffn_chunk(c, c % 2)
            scales(2)
            with v.Fori(0, NC) as c:
                norm(c, lambda tt, n: res[:, bass.ds(n, 1), :].rearrange("p a n -> p (a n)"), o_ready, NC)


_INPUTS = ("xt", "x", "w_qk", "b_qk", "w_v", "w_line", "b_v", "b_gate", "inc", "out_w", "out_b", "wg", "wu", "wd")


def kernel(**inputs):
    import numpy as np
    import concourse.bacc as bacc
    from concourse.bass_utils import run_bass_kernel_spmd as run

    a = {k[3:]: np.asarray(v) for k, v in inputs.items()}
    x = a["attn_x"].reshape(B * T, D)
    padded = np.zeros((B, D, T + 1), x.dtype)
    padded[:, :, 1:] = x.reshape(B, T, D).transpose(0, 2, 1)
    xt = np.stack([padded[c // CPB, :, (c % CPB) * CH:(c % CPB) * CH + CH + 1] for c in range(NC)])
    qkv_w, qkv_b = a["attn_qkv_w"], a["attn_qkv_b"]
    laid = {
        "xt": xt, "x": x,
        "w_qk": qkv_w[:, :2 * D], "b_qk": qkv_b[:2 * D].reshape(4, P).T,
        "w_v": np.concatenate([qkv_w[:, 2 * D:], a["attn_geo_w"]], 1),
        "w_line": np.concatenate([a["attn_w1_write"], a["attn_w2_write"], a["attn_w1_read"],
                                  a["attn_w2_read"], a["attn_gate_w"]], 1),
        "b_v": np.concatenate([qkv_b[2 * D:], a["attn_geo_b"]]), "b_gate": a["attn_gate_b"],
        "inc": a["attn_inc_scale"], "out_w": a["attn_out_w"], "out_b": a["attn_out_b"],
        "wg": a["ffn_w_gate"].T, "wu": a["ffn_w_up"].T, "wd": a["ffn_w_down"].T,
    }
    nc = bacc.Bacc("TRN2", target_bir_lowering=False, num_devices=1)
    arrays, args = {}, []
    for name in _INPUTS:
        arr = np.ascontiguousarray(laid[name])
        arrays[f"in_{name}"] = arr
        args.append(nc.dram_tensor(f"in_{name}", arr.shape, mybir.dt.from_np(arr.dtype), kind="ExternalInput").ap())
    out = nc.dram_tensor("out_0", (B * T, D), F32, kind="ExternalOutput").ap()
    build(nc, *args, out)
    r = run(nc, [arrays], core_ids=[0])
    return r.results[0]["out_0"].reshape(B, T, D)
```

```python
import concourse.bass as bass
from concourse import mybir
from contextlib import ExitStack

F32 = mybir.dt.float32
BF16 = mybir.dt.bfloat16
I32 = mybir.dt.int32
ALU = mybir.AluOpType
ACT = mybir.ActivationFunctionType
AX = mybir.AxisListType

P = 128
B, T, D, H = 2, 2048, 256, 16
DH = D // H
HID = 768
NK = D // P
CH = 512
NC = B * T // CH
CPB = T // CH
TT = CH // P
NPART = 3
PAIRS = [(0, 1), (0, 2), (0, 3), (1, 2), (1, 3), (2, 3)]
NCOMP = len(PAIRS)
J_SIGN = [1, -1, 1, 1, -1, 1]
SCALE_Q = float(DH) ** -0.5
SCALE_W = 1.0 / 127.0
EPS = 1e-5
MASKED = -1.0e38
GEO_SAFE = 60.0
GEO, DOT = 0, 1
ORDER = (1, 0)

HG = 4
NG = H // HG
NPAIR = B * NG
ITEMS = 2 * NPAIR
NKB = T // P
NQT = T // CH
Q_PARTS = [0, 0, 1, 1, 0, 2]
K_PARTS = [0, 1, 0, 1, 2, 0]
NROW = DH * len(Q_PARTS)
NROWM = NROW + 2
VW = 32


def steps():
    out = []
    for qt in range(NQT):
        for kb in range(0, TT * qt, 2):
            out.append((qt, [(kb, CH), (kb + 1, CH)]))
        for j in (0, 2):
            out.append((qt, [(TT * qt + j, CH - P * j), (TT * qt + j + 1, CH - P * (j + 1))]))
    return out


STEPS = steps()
NSTEP = len(STEPS)
NEX = NSTEP * HG
DIAGONAL = [s for s, x in enumerate(STEPS) if x[1][0][0] >= TT * x[0]]
FIRST_OF = {qt: min(s for s, x in enumerate(STEPS) if x[0] == qt) for qt in range(NQT)}
LAST_OF = {qt: max(s for s, x in enumerate(STEPS) if x[0] == qt) for qt in range(NQT)}


def place(s):
    (_, w0), (_, w1) = STEPS[s][1]
    second = CH if w0 + w1 > CH else w0
    return (0, second), second + w1


def max_tiles():
    out = []
    for h in range(HG):
        for qb in range(NKB):
            end = (qb + 1) * P
            for k0 in range(0, end, CH):
                out.append((h, qb, k0, min(CH, end - k0), k0 + CH >= end))
    return out


MAXT = max_tiles()
NMT = len(MAXT)
NMX = NMT + 1
MT_STEP = NSTEP - 2


def spread(steps_of):
    size = [sum(w for _, w in STEPS[s][1]) + 2 * P if s >= 0 else 0 for s in steps_of]
    cols = [w + (P if d else 0) for _, _, _, w, d in MAXT]
    out, u, done = [], 0, 0
    for i in range(len(steps_of)):
        mine = []
        while u < NMT and done + cols[u] / 2 <= sum(cols) * sum(size[:i + 1]) / sum(size):
            mine.append(u)
            done += cols[u]
            u += 1
        out.append(mine)
    assert u == NMT
    return out


_REST = [-1] * (NSTEP - MT_STEP)
_TWO = spread([s for s in range(MT_STEP)] + _REST + [s for s in range(MT_STEP)] + _REST)
MAX_IN_DOT, MAX_IN_GEO = _TWO[:NSTEP], _TWO[NSTEP:]
MAX_IN_FIRST = spread([-1] * 3 + [s for s in range(3, MT_STEP)] + _REST)
WHERE = [(), (5,), (1, 4), (1, 3, 5), (0, 1, 3, 5), (0, 1, 3, 4, 5), (0, 1, 2, 3, 4, 5)]
COUNT = (2, 1)
NO_MAXIMA = [[] for _ in range(NSTEP)]
MAX_BEFORE = sum(len(u) for u in MAX_IN_DOT)


def build(nc, xt, x, w_qk, b_qk, w_v, w_line, b_v, b_gate, inc, out_w, out_b, wg, wu, wd, out):
    ctx = ExitStack()
    with ctx:
        parts = nc.dram_tensor("parts", (2, 2, B, NPART, H * DH, T), BF16).ap()
        values = nc.dram_tensor("values", (ITEMS, P, NKB, HG * VW), F32).ap()
        heads = nc.dram_tensor("heads", (ITEMS, P, NKB, HG * DH), F32).ap()

        def sb(name, shape, dt=F32):
            return ctx.enter_context(nc.sbuf_tensor(name, shape, dt))

        ident = sb("ident", [P, P])
        ident16 = sb("ident16", [P, P], BF16)
        mask_qk = sb("mask_qk", [P, P], BF16)
        gate_z = sb("gate_z", [P, NC * TT, H])
        wide = sb("wide", [P, 1], I32)
        weights = {
            "int": sb("w_int", [P, NK * HID], I32), "gate": sb("wg_f", [P, NK, HID]),
            "up": sb("wu_f", [P, NK, HID]), "down": sb("wd_f", [P, HID // P, D]),
            "out": sb("wo", [P, NK, D]), "out_b": sb("ob", [P, D])}
        first = {
            "q": sb("qa0", [P, HG, T], BF16), "k": sb("ka0", [P, HG, T], BF16),
            "v": sb("va0", [P, NKB, HG * VW]),
            "qk_in": [ctx.enter_context(nc.semaphore(f"qk_in0_{j}")) for j in range(2)],
            "v_in": ctx.enter_context(nc.semaphore("v_in0"))}
        project(nc, xt, w_qk, b_qk, w_v, w_line, b_v, b_gate, inc, parts, values, first,
                ident, ident16, mask_qk, gate_z, wide)
        attend(nc, parts, values, heads, ident, ident16, mask_qk, wide,
               out_w, out_b, wg, wu, wd, weights, first)
        finish(nc, x, heads, gate_z, ident, weights, out)


def load_operands(q, parts, p, kind, q_set, k_set, loaded, which=range(4 * NCOMP)):
    b, g = p // NG, p % NG
    for i in which:
        j, side, n = i // (2 * NCOMP), (i // NCOMP) % 2, i % NCOMP
        src = parts[side, kind, b, (Q_PARTS, K_PARTS)[side][n], bass.ds(g * (HG * DH) + j * 2 * DH, 2 * DH), :]
        q.dma_start((q_set, k_set)[side][n * DH:(n + 1) * DH, 2 * j:2 * j + 2, :],
                    src.rearrange("(h d) t -> d h t", h=2)).then_inc(loaded[j], 16)


def project(nc, xt, w_qk, b_qk, w_v, w_line, b_v, b_gate, inc, parts, values, first,
            ident, ident16, mask_qk, gate_z, wide):
    LN_WRITES = 1 + NCOMP
    LINKS = 7
    NR = 8
    LINE = 4 * H * 4
    NLN = TT * 2 * H
    with ExitStack() as ctx:
        def sb(name, shape, dt=F32):
            return ctx.enter_context(nc.sbuf_tensor(name, shape, dt))

        def pb(name, shape):
            return ctx.enter_context(nc.psum_tensor(name, shape, F32))

        def sem(name):
            return ctx.enter_context(nc.semaphore(name))

        wqk = sb("wqk", [P, NK, 2 * D])
        wv = sb("wv", [P, NK, 2 * D])
        wl = sb("wl", [P, NK, LINE + H])
        bqk = sb("bqk", [P, 4])
        bqs = sb("bqs", [P, 4])
        bv = sb("bv", [P, 2 * D])
        bg = sb("bg", [P, H])
        incb = sb("incb", [P, H])
        xc = [sb(f"xc{i}", [P, NK, CH + 1]) for i in range(2)]
        vn = [sb(f"vn{i}", [P, 2 * H, VW]) for i in range(TT)]
        gs = sb("gs", [P, 2, TT * 2, H * 4])
        gz = sb("gz", [P, TT, H])
        prod_a = sb("prod_a", [P, NLN, NCOMP])
        prod_b = sb("prod_b", [P, NLN, NCOMP])
        line = sb("line", [P, NLN, NCOMP])
        sq = sb("sq", [P, NLN, NCOMP])
        sum6 = sb("sum6", [P, NLN])
        ss = sb("ss", [P, NLN])
        nrm = sb("nrm", [P, NLN])
        rn = sb("rn", [P, TT, 2, H])
        rinc = sb("rinc", [P, TT, H])
        rneg = sb("rneg", [P, TT, H])
        most = sb("most", [P, 1])
        ln = sb("ln", [P, TT, 2, H, DH])
        t32 = [sb(f"t32_{i}", [P, CH]) for i in range(4)]
        d32 = [sb(f"d32_{i}", [P, CH]) for i in range(4)]
        sp3 = [sb(f"sp3_{i}", [P, NPART, CH], BF16) for i in range(NR)]
        pn = [pb(f"pn{i}", [P, 2, CH]) for i in range(2)]
        pr = [pb(f"pr{i}", [P, CH]) for i in range(4)]

        w_in = sem("w_in")
        x_in = [sem(f"x_in{i}") for i in range(2)]
        n_ready = sem("n_ready")
        v_out = sem("v_out")
        g_out = sem("g_out")
        v_st = [sem(f"v_st{i}") for i in range(TT)]
        rows_ready = sem("rows_ready")
        row_act = sem("row_act")
        d_done = sem("d_done")
        p2_done = sem("p2_done")
        p3_done = sem("p3_done")
        s_st = [sem(f"s_st{i}") for i in range(NR)]
        ss_ready = sem("ss_ready")
        nrm_ready = sem("nrm_ready")
        ln_ready = sem("ln_ready")
        vn_ready = sem("vn_ready")
        wv_in = sem("wv_in")
        id_ready = sem("id_ready")
        passed = sem("sp_passed1")
        wide_ready = sem("wide_ready")
        ones_in = sem("ones_in")
        dve = sem("dve")
        block = ctx.enter_context(nc.Block())

        @block.sync
        def _(q):
            q.dma_start(xc[0][:, :, :], xt[0].rearrange("(k p) t -> p k t", p=P)).then_inc(x_in[0], 16)
            q.dma_start(wv[:, :, :], w_v.rearrange("(k p) n -> p k n", p=P)).then_inc(wv_in, 16)
            q.dma_start(wl[:, :, :], w_line.rearrange("(k p) n -> p k n", p=P)).then_inc(w_in, 16)
            q.dma_start(wqk[:, :, :], w_qk.rearrange("(k p) n -> p k n", p=P)).then_inc(w_in, 16)
            q.dma_start(xc[1][:, :, :], xt[1].rearrange("(k p) t -> p k t", p=P)).then_inc(x_in[1], 16)

            def store_v(c, tt):
                q.wait_ge(v_out, c * TT + tt + 1)
                q.sem_inc(passed, 1)
                dst = values[:, :, :, :].rearrange("(b g a) p k n -> a b k p g n", a=2, b=B)
                for a in range(2):
                    q.dma_start(dst[ORDER[a], c // CPB, (c % CPB) * TT + tt, :, :, :],
                                vn[tt][:, a * H:(a + 1) * H, :].rearrange("p (g h) w -> p g (h w)", g=NG))\
                     .then_inc(v_st[tt], 16)

            def store_row(c, m):
                q.wait_ge(p3_done, c * NR + m + 1)
                q.sem_inc(passed, 1)
                q.dma_start(
                    parts[(m // 2) % 2, ORDER[m // 4], c // CPB, :, (m % 2) * P:(m % 2 + 1) * P,
                          bass.ds((c % CPB) * CH, CH)].rearrange("s r t -> r s t"),
                    sp3[m][:, :, :]).then_inc(s_st[m], 16)

            def load_x(c, par):
                q.wait_ge(rows_ready, (c - 2) * NR + 4)
                q.sem_inc(passed, 1)
                q.dma_start(xc[par][:, :, :], xt[c].rearrange("(k p) t -> p k t", p=P)).then_inc(x_in[par], 16)

            def stores(c):
                for tt in range(TT):
                    store_v(c, tt)
                    store_row(c - 1, tt)
                for m in range(4, NR):
                    store_row(c - 1, m)

            for tt in range(TT):
                store_v(0, tt)
            with q.Fori(0, NC // 2 - 2) as k:
                for par in range(2):
                    c = 2 * k + 1 + par
                    load_x(c + 1, par)
                    stores(c)
            load_x(NC - 2, 0)
            stores(NC - 3)
            load_x(NC - 1, 1)
            for m in range(4, NR):
                q.wait_ge(s_st[m], CPB * 16)
            for tt in range(TT):
                q.wait_ge(v_st[tt], CPB * 32)
            for tt in range(TT):
                store_v(NC - 2, tt)
                store_row(NC - 3, tt)
                load_operands(q, parts, 0, GEO, first["q"], first["k"], first["qk_in"], range(3 * tt, 3 * tt + 3))
            for m in range(4, NR):
                store_row(NC - 3, m)
                load_operands(q, parts, 0, GEO, first["q"], first["k"], first["qk_in"], range(3 * m, 3 * m + 3))
            q.dma_start(first["v"][:, :, :], values[0]).then_inc(first["v_in"], 16)
            stores(NC - 1)
            for m in range(NR):
                store_row(NC - 1, m)
            for tt in range(TT):
                q.wait_ge(v_st[tt], NC * 32)
            for m in range(NR):
                q.wait_ge(s_st[m], NC * 16)

        @block.gpsimd
        def _(g):
            g.memset(ident[:, :], 0.0).then_inc(id_ready, 1)
            g.memset(ident16[:, :], 0.0).then_inc(id_ready, 1)
            g.memset(mask_qk[:, :], 0.0).then_inc(id_ready, 1)
            g.memset(ln[:, :, :, :, :], 0.0).then_inc(id_ready, 1)
            g.wait_ge(id_ready, 4)
            for m in (ident, ident16):
                g.affine_select(out=m[:, :], in_=m[:, :], compare_op=ALU.not_equal, fill=1.0, base=0,
                                pattern=[[-1, P]], channel_multiplier=1).then_inc(id_ready, 1)
            g.affine_select(out=mask_qk[:, :], in_=mask_qk[:, :], compare_op=ALU.is_ge, fill=MASKED,
                            base=0, pattern=[[-1, P]], channel_multiplier=1).then_inc(id_ready, 1)
            g.wait_ge(id_ready, 7)
            g.memset(first["k"][NROW:NROWM, :, :], 1.0).then_inc(ones_in, 1)
            g.wait_ge(ones_in, 1)
            with g.Fori(0, NC) as c:
                for m in range(NR):
                    g.wait_ge(p2_done, c * NR + m + 1)
                    g.tensor_tensor(out=sp3[m][:, 2, :], in0=d32[m % 4][:, :],
                                    in1=sp3[m][:, 1, :], op=ALU.subtract).then_inc(p3_done, 1)

        @block.tensor
        def _(pe):
            pe.wait_ge(wv_in, 16)

            def token_tiles(c, par, loads, head):
                pe.wait_ge(x_in[par], loads * 16)
                for tt in range(TT):
                    if not (head and tt < 2):
                        pe.wait_ge(v_out, c * TT + tt - 1)
                        pe.wait_ge(g_out, (c * TT + tt - 1) * 2)
                    tok = slice(1 + tt * P, 1 + (tt + 1) * P)
                    prev = slice(tt * P, (tt + 1) * P)
                    bank = pn[tt % 2]
                    for k in range(NK):
                        pe.matmul(bank[:, 0, :], xc[par][:, k, tok], wv[:, k, :], start=k == 0, stop=k == NK - 1)
                    if head and tt == 0:
                        pe.wait_ge(w_in, 6 * 16)
                    for k in range(NK):
                        pe.matmul(bank[:, 1, 0:H * 4], xc[par][:, k, prev], wl[:, k, 0:H * 4],
                                  start=k == 0, stop=k == NK - 1)
                    for k in range(NK):
                        last = pe.matmul(bank[:, 1, H * 4:LINE + H], xc[par][:, k, tok], wl[:, k, H * 4:],
                                         start=k == 0, stop=k == NK - 1)
                    last.then_inc(n_ready, 1)

            def qk_rows(c, par, head):
                for m in range(4):
                    if not head:
                        pe.wait_ge(row_act, (c * NR + m - 3) * 2)
                    for k in range(NK):
                        last = pe.matmul(pr[m][:, :], wqk[:, k, m * P:(m + 1) * P], xc[par][:, k, 1:],
                                         start=k == 0, stop=k == NK - 1)
                    last.then_inc(rows_ready, 1)

            def line_rows(c):
                pe.wait_ge(ln_ready, (c + 1) * LN_WRITES)
                for m in range(4, NR):
                    pe.wait_ge(row_act, (c * NR + m - 3) * 2)
                    for tt in range(TT):
                        src = ln[:, tt, (m - 4) // 2, (m % 2) * 8:(m % 2) * 8 + 8, :]
                        last = pe.transpose(pr[m % 4][:, tt * P:(tt + 1) * P],
                                            src.rearrange("p h d -> p (h d)"), ident[:, :])
                    last.then_inc(rows_ready, 1)

            token_tiles(0, 0, 1, True)
            qk_rows(0, 0, True)
            token_tiles(1, 1, 1, False)
            pe.wait_ge(id_ready, 7)
            line_rows(0)
            qk_rows(1, 1, False)
            with pe.Fori(1, NC // 2) as k:
                for par in range(2):
                    c = 2 * k + par
                    token_tiles(c, par, k + 1, False)
                    line_rows(c - 1)
                    qk_rows(c, par, False)
            line_rows(NC - 1)

        @block.scalar
        def _(act):
            act.dma_start(bqk[:, :], b_qk).then_inc(w_in, 16)
            act.dma_start(bv[:, :], b_v.partition_broadcast(P)).then_inc(w_in, 16)
            act.dma_start(bg[:, :], b_gate.partition_broadcast(P)).then_inc(w_in, 16)
            act.dma_start(incb[:, :], inc.partition_broadcast(P)).then_inc(w_in, 16)
            act.wait_ge(dve, 2)

            def row_in(c, m, head):
                bias = bqs[:, m:m + 1] if m < 4 else 0.0
                scale = SCALE_Q if m < 2 else 1.0
                act.wait_ge(rows_ready, c * NR + m + 1)
                if not (head and m < 4):
                    act.wait_ge(d_done, c * NR + m - 3)
                if not head:
                    act.wait_ge(s_st[m], c * 16)
                act.activation(t32[m % 4][:, :], pr[m % 4][:, :], ACT.Identity, bias=bias, scale=scale)\
                   .then_inc(row_act, 1)
                act.activation(sp3[m][:, 0, :], pr[m % 4][:, :], ACT.Identity, bias=bias, scale=scale)\
                   .then_inc(row_act, 1)

            def second_part(c, m):
                act.wait_ge(d_done, c * NR + m + 1)
                act.activation(sp3[m][:, 1, :], d32[m % 4][:, :], ACT.Copy).then_inc(p2_done, 1)

            def points(c, tt, head):
                act.wait_ge(n_ready, c * TT + tt + 1)
                if tt == 0 and not head:
                    act.wait_ge(dve, (c - 1) * LINKS + 4)
                bank = pn[tt % 2][:, 1, :]
                act.activation(gs[:, :, 2 * tt:2 * tt + 2, :],
                               bank[:, 0:LINE].rearrange("p (y w n) -> p w y n", y=2, w=2),
                               ACT.Copy).then_inc(g_out, 1)
                act.activation(gz[:, tt, :], bank[:, LINE:LINE + H], ACT.Copy).then_inc(g_out, 1)

            def lengths(c):
                act.wait_ge(ss_ready, c + 1)
                act.activation(nrm[:, :], ss[:, :], ACT.Sqrt).then_inc(nrm_ready, 1)

            def line_rows(c, head):
                for m in range(4, NR):
                    row_in(c, m, head)
                    if m > 4:
                        second_part(c, m - 1)
                second_part(c, NR - 1)

            def chunk(c, head, second):
                for tt in range(TT):
                    points(c, tt, head)
                    if not head:
                        second_part(c - 1, tt)
                if not head:
                    line_rows(c - 1, second)
                for m in range(4):
                    row_in(c, m, head)
                lengths(c)

            chunk(0, True, False)
            chunk(1, False, True)
            with act.Fori(2, NC) as c:
                chunk(c, False, False)
            for m in range(4):
                second_part(NC - 1, m)
            line_rows(NC - 1, False)

        @block.vector
        def _(v):
            for i in range(TT):
                v.memset(vn[i][:, :, :], 0.0).then_inc(vn_ready, 1)
            v.wait_ge(vn_ready, TT)
            for i in range(TT):
                v.memset(vn[i][:, :, DH:DH + 1], 1.0).then_inc(vn_ready, 1)
            v.wait_ge(vn_ready, 2 * TT)
            v.wait_ge(w_in, 6 * 16)
            v.tensor_scalar(bqs[:, 0:2], bqk[:, 0:2], SCALE_Q, None, ALU.mult).then_inc(dve, 1)
            v.tensor_copy(bqs[:, 2:4], bqk[:, 2:4]).then_inc(dve, 1)
            v.tensor_reduce(out=most[:, :], in_=incb[:, :], axis=AX.X, op=ALU.max,
                            apply_absolute_value=True).then_inc(dve, 1)
            v.wait_ge(dve, 3)
            v.tensor_scalar(wide[:, :], most[:, :], GEO_SAFE, None, ALU.is_gt).then_inc(wide_ready, 1)
            p1, p2 = (gs[:, w, :, :].rearrange("p y (h c) -> p (y h) c", c=4) for w in range(2))
            line_v = line[:, :, :].rearrange("p (t y h) c -> p t y h c", t=TT, y=2)

            def first_rest(c, m, head):
                v.wait_ge(row_act, (c * NR + m + 1) * 2)
                if not (head and m < 4):
                    v.wait_ge(p3_done, c * NR + m - 3)
                v.tensor_tensor(out=d32[m % 4][:, :], in0=t32[m % 4][:, :], in1=sp3[m][:, 0, :],
                                op=ALU.subtract).then_inc(d_done, 1)

            def chunk(c, head, second):
                base = c * LINKS + 3
                for tt in range(TT):
                    v.wait_ge(n_ready, c * TT + tt + 1)
                    if not head:
                        v.wait_ge(v_st[tt], c * 32)
                    v.tensor_tensor(out=vn[tt][:, :, 0:DH],
                                    in0=pn[tt % 2][:, 0, :].rearrange("p (h d) -> p h d", d=DH),
                                    in1=bv[:, :].rearrange("p (h d) -> p h d", d=DH),
                                    op=ALU.add).then_inc(v_out, 1)
                    if not head:
                        first_rest(c - 1, tt, second)
                if not head:
                    for m in range(4, NR):
                        first_rest(c - 1, m, second)
                v.wait_ge(g_out, (c + 1) * TT * 2)
                v.tensor_tensor(out=gate_z[:, bass.ds(c * TT, TT), :], in0=gz[:, :, :],
                                in1=bg[:, :].unsqueeze(1).to_broadcast([P, TT, H]), op=ALU.add)
                o = 0
                for i in range(3):
                    n = 3 - i
                    v.tensor_tensor(out=prod_a[:, :, o:o + n], in0=p1[:, :, i:i + 1].to_broadcast([P, NLN, n]),
                                    in1=p2[:, :, i + 1:4], op=ALU.mult)
                    last = v.tensor_tensor(out=prod_b[:, :, o:o + n], in0=p1[:, :, i + 1:4],
                                           in1=p2[:, :, i:i + 1].to_broadcast([P, NLN, n]), op=ALU.mult)
                    o += n
                last.then_inc(dve, 1)
                v.wait_ge(dve, base + 1)
                v.tensor_tensor(out=line[:, :, :], in0=prod_a[:, :, :], in1=prod_b[:, :, :],
                                op=ALU.subtract).then_inc(dve, 1)
                v.wait_ge(dve, base + 2)
                v.tensor_tensor(out=sq[:, :, :], in0=line[:, :, :], in1=line[:, :, :], op=ALU.mult)\
                 .then_inc(dve, 1)
                v.wait_ge(dve, base + 3)
                v.tensor_reduce(out=sum6[:, :], in_=sq[:, :, :], axis=AX.X, op=ALU.add).then_inc(dve, 1)
                v.wait_ge(dve, base + 4)
                if not head:
                    v.wait_ge(nrm_ready, c)
                v.tensor_scalar(ss[:, :], sum6[:, :], 1e-24, None, ALU.max).then_inc(ss_ready, 1)
                v.wait_ge(nrm_ready, c + 1)
                v.reciprocal(rn[:, :, :, :].rearrange("p t y h -> p (t y h)"), nrm[:, :]).then_inc(dve, 1)
                v.wait_ge(dve, base + 5)
                v.tensor_tensor(out=rinc[:, :, :], in0=rn[:, :, 1, :],
                                in1=incb[:, :].unsqueeze(1).to_broadcast([P, TT, H]), op=ALU.mult)\
                 .then_inc(dve, 1)
                v.wait_ge(dve, base + 6)
                v.tensor_scalar(rneg[:, :, :], rinc[:, :, :], -1.0, None, ALU.mult).then_inc(dve, 1)
                v.wait_ge(dve, base + 7)
                if head:
                    v.wait_ge(id_ready, 7)
                else:
                    v.wait_ge(rows_ready, c * NR)
                v.tensor_tensor(
                    out=ln[:, :, 1, :, 0:NCOMP], in0=line_v[:, :, 0, :, :],
                    in1=rn[:, :, 0, :].unsqueeze(3).to_broadcast([P, TT, H, NCOMP]),
                    op=ALU.mult).then_inc(ln_ready, 1)
                for i in range(NCOMP):
                    v.tensor_tensor(out=ln[:, :, 0, :, NCOMP - 1 - i], in0=line_v[:, :, 1, :, i],
                                    in1=(rinc if J_SIGN[i] > 0 else rneg)[:, :, :],
                                    op=ALU.mult).then_inc(ln_ready, 1)

            chunk(0, True, False)
            chunk(1, False, True)
            with v.Fori(2, NC) as c:
                chunk(c, False, False)
            for m in range(NR):
                first_rest(NC - 1, m, False)


def attend(nc, parts, values, heads, ident, ident16, mask_qk, wide, out_w, out_b, wg, wu, wd, weights,
           first):
    with ExitStack() as ctx:
        def sb(name, shape, dt=F32):
            return ctx.enter_context(nc.sbuf_tensor(name, shape, dt))

        def pb(name, shape):
            return ctx.enter_context(nc.psum_tensor(name, shape, F32))

        def sem(name):
            return ctx.enter_context(nc.semaphore(name))

        qa = [first["q"]] + [sb(f"qa{i}", [P, HG, T], BF16) for i in (1, 2)]
        ka = [first["k"]] + [sb(f"ka{i}", [P, HG, T], BF16) for i in (1, 2)]
        va = [first["v"], sb("va1", [P, NKB, HG * VW])]
        prob = [sb(f"prob{i}", [P, 2 * CH]) for i in range(8)]
        ot = [sb(f"ot{i}", [P, CH]) for i in range(2)]
        rz = sb("rz", [P, TT * HG])
        on = [sb(f"on{i}", [P, TT, HG * DH]) for i in range(2)]
        mp = [sb(f"mp{i}", [P, HG * NKB, NKB * P // CH]) for i in range(2)]
        negm = sb("negm", [P, P])
        mrow = sb("mrow", [HG * NKB, 2, P], BF16)
        ex = pb("ex", [P, 2, 2 * CH])
        mx = pb("mx", [P, 2, CH])
        pv = pb("pv", [P, 2, CH])

        qk_in = [first["qk_in"]] + [[sem(f"qk_in{i}_{j}") for j in range(2)] for i in (1, 2)]
        v_in = [first["v_in"], sem("v_in1")]
        m_in = sem("m_in")
        ones_ready = sem("ones_ready")
        ex_ready = sem("ex_ready")
        ex_done = sem("ex_done")
        pv_step = sem("pv_step")
        ot_ready = sem("ot_ready")
        tr_done = sem("tr_done")
        rz_ready = sem("rz_ready")
        on_ready = sem("on_ready")
        on_st = [sem(f"on_st{i}") for i in range(2)]
        mx_ready = [sem(f"mx_ready{i}") for i in range(2)]
        mx_free = [sem(f"mx_free{i}") for i in range(2)]
        negm_ready = [sem(f"negm_ready{i}") for i in range(2)]
        mrow_ready = sem("mrow_ready")
        masked = sem("masked")
        g_passed = sem("g_passed")
        w_load = sem("w_load")
        w_conv = sem("w_conv")
        passed = sem("sp_passed2")
        block = ctx.enter_context(nc.Block())

        @block.sync
        def _(q):
            def load_qk(p, kind, which):
                load_operands(q, parts, p, kind, qa[which], ka[which], qk_in[which])

            def load_v(it, kind):
                q.dma_start(va[kind][:, :, :], values[it]).then_inc(v_in[kind], 16)

            def store(it, qt):
                q.wait_ge(on_ready, it * NQT + qt + 1)
                q.sem_inc(passed, 1)
                q.dma_start(heads[it, :, qt * TT:(qt + 1) * TT, :],
                            on[qt % 2][:, :, :]).then_inc(on_st[qt % 2], 16)

            def rows(it, which):
                q.wait_ge(mrow_ready, it + 1)
                q.sem_inc(passed, 1)
                for i in range(2):
                    q.dma_start(qa[which][NROW + i:NROW + i + 1, :, :].rearrange("p h (k t) -> p (h k) t", t=P),
                                mrow[:, i, :]).then_inc(m_in, 16)

            def item(p, kind, par, first, last):
                it = 2 * p + kind
                head, tail = first and kind == GEO, last and kind == DOT
                if not (last or tail):
                    if not head:
                        q.wait_ge(ex_ready, it * NEX)
                        q.sem_inc(passed, 1)
                    load_qk(p + 1, 1 - kind, 2 - par if kind == GEO else 0)
                if not head:
                    store(it - 1, NQT - 1)
                if not tail:
                    if not head:
                        q.wait_ge(pv_step, it * NSTEP)
                        q.sem_inc(passed, 1)
                    load_v(it + 1, 1 - kind)
                for qt in range(NQT - 1):
                    store(it, qt)
                if not tail:
                    rows(it + 1, 1 + par if kind == GEO else 0)

            def pair(p, par, first, last):
                item(p, GEO, par, first, last)
                item(p, DOT, par, first, last)

            rows(0, 0)
            load_qk(0, DOT, 1)
            pair(0, 0, True, False)
            with q.Fori(0, NPAIR // 2 - 1) as k:
                pair(2 * k + 1, 1, False, False)
                pair(2 * k + 2, 0, False, False)
            pair(NPAIR - 1, 1, False, True)
            store(ITEMS - 1, NQT - 1)
            for i in range(2):
                q.wait_ge(on_st[i], ITEMS * NQT // 2 * 16)

        @block.gpsimd
        def _(g):
            g.memset(negm[:, :], 0.0).then_inc(ones_ready, 1)
            for i in range(2):
                g.wait_ge(ones_ready, i + 1)
                g.memset(mp[i][:, :, :], MASKED).then_inc(ones_ready, 1)
            g.wait_ge(ones_ready, 3)
            ffn = [(weights[n], src, weights["int"][:, :].rearrange("p (k n) -> p k n", k=src.shape[0] // P))
                   for n, src in (("gate", wg), ("up", wu), ("down", wd))]

            def load_weight(i):
                _, src, raw = ffn[i]
                g.dma_start(raw, src.rearrange("(k p) n -> p k n", p=P)).then_inc(w_load, 16)

            def convert_weight(i):
                dst, _, raw = ffn[i]
                g.wait_ge(w_load, (i + 3) * 16)
                g.tensor_copy(dst[:, :, :], raw).then_inc(w_conv, 1)
                g.wait_ge(w_conv, i + 1)

            def aside(it):
                if it == 0:
                    for i in (1, 2):
                        g.wait_ge(masked, (len(DIAGONAL) - TT // 2) * HG)
                        g.wait_ge(ones_ready, i + 2)
                        g.memset(ka[i][NROW:NROWM, :, :], 1.0).then_inc(ones_ready, 1)
                    g.wait_ge(ones_ready, 5)
                    g.dma_start(weights["out"][:, :, :], out_w.rearrange("(k p) n -> p k n", p=P))\
                     .then_inc(w_load, 16)
                    g.dma_start(weights["out_b"][:, :], out_b.partition_broadcast(P)).then_inc(w_load, 16)
                    g.wait_ge(w_load, 32)
                else:
                    convert_weight(it - 1)
                if it < len(ffn):
                    load_weight(it)

            def item(it, has_aside):
                for s in DIAGONAL:
                    (_, second), _ = place(s)
                    for h in range(HG):
                        n = s * HG + h
                        g.wait_ge(ex_done, it * NEX + n + 1)
                        g.sem_inc(g_passed, 1)
                        two = prob[n % 8][:, 0:2 * second].rearrange("p (b c) -> p b c", b=2)[:, :, 0:P]
                        g.affine_select(out=two, in_=two, compare_op=ALU.is_ge, fill=0.0, base=0,
                                        pattern=[[0, 2], [1, P]], channel_multiplier=-1).then_inc(masked, 1)
                    if has_aside and s == LAST_OF[NQT - 2]:
                        aside(it)

            for it in range(len(ffn) + 1):
                item(it, True)
            with g.Fori(len(ffn) + 1, ITEMS) as it:
                item(it, False)

        @block.tensor
        def _(pe):
            is_wide = pe.value_load(wide[0:1, 0:1], min_val=0, max_val=1)

            def scores(it, which, s, h, head):
                n = s * HG + h
                slot = n % 2
                if not (head and n < 2):
                    pe.wait_ge(ex_done, it * NEX + n - 1)
                qt, blocks = STEPS[s]
                at, _ = place(s)
                for (kb, w), c0 in zip(blocks, at):
                    dst = ex[:, slot, c0:c0 + w]
                    last = pe.matmul(dst, ka[which][0:NROWM, h, kb * P:(kb + 1) * P],
                                     qa[which][0:NROWM, h, (qt + 1) * CH - w:(qt + 1) * CH],
                                     start=True, stop=True)
                last.then_inc(ex_ready, 1)

            def max_tile(p, kind, which, use, u):
                h, qb, k0, w, on_diagonal = MAXT[u]
                if qb == 0 and h % 2 == 0:
                    pe.wait_ge(qk_in[which][h // 2], use * 12 * 16)
                if u >= 2:
                    pe.wait_ge(mx_free[kind], p * (NMX * COUNT[kind]) + (u - 1) * COUNT[kind])
                dst = mx[:, u % 2, 0:w]
                last = pe.matmul(dst, qa[which][0:NROW, h, qb * P:(qb + 1) * P],
                                 ka[which][0:NROW, h, k0:k0 + w], start=True, stop=not on_diagonal)
                if on_diagonal:
                    last = pe.matmul(dst[:, w - P:w], ident16[:, :], mask_qk[:, :], start=False, stop=True)
                last.then_inc(mx_ready[kind], COUNT[kind])

            def max_rows(p, kind):
                pe.wait_ge(negm_ready[kind], p + 1)
                pe.transpose(mx[:, 0, 0:P], negm[:, :], ident[:, :]).then_inc(mx_ready[kind], COUNT[kind])

            def wide_maxima(p):
                with pe.If(is_wide > 0):
                    for u in range(NMT):
                        max_tile(p, GEO, 0, p + 1, u)
                    max_rows(p, GEO)

            def times_v(it, kind, s, j, head):
                qt, blocks = STEPS[s]
                kb, w = blocks[j]
                at, _ = place(s)
                if j == 0:
                    if s in DIAGONAL:
                        pe.wait_ge(masked, (it * len(DIAGONAL) + DIAGONAL.index(s) + 1) * HG)
                    else:
                        pe.wait_ge(ex_done, it * NEX + s * HG + HG)
                    if s == 0:
                        pe.wait_ge(v_in[kind], (it // 2 + 1) * 16)
                    if s == FIRST_OF[qt] and not (head and qt < 2):
                        pe.wait_ge(on_ready, it * NQT + qt - 1)
                end = j == 1 and s == LAST_OF[qt]
                for h in range(HG):
                    last = pe.matmul(pv[h * VW:(h + 1) * VW, qt % 2, CH - w:CH],
                                     va[kind][:, kb, h * VW:(h + 1) * VW],
                                     prob[(s * HG + h) % 8][:, at[j]:at[j] + w],
                                     start=kb == 0, stop=end, tile_position=(0, h * VW))
                if j == 1:
                    last.then_inc(pv_step, 1)

            def turn(it, qt):
                pe.wait_ge(ot_ready, it * NQT + qt + 1)
                for i in range(TT):
                    last = pe.transpose(pv[:, qt % 2, i * P:(i + 1) * P], ot[qt % 2][:, i * P:(i + 1) * P],
                                        ident[:, :])
                last.then_inc(tr_done, 1)

            def step(p, kind, par, s, head, maxima, last):
                it = 2 * p + kind
                which = 1 + par if kind == DOT else 0
                mp_of, mpar = (p, par) if kind == GEO else (p + 1, 1 - par)
                later = list(maxima[s])
                where = [WHERE[min(len(later), 6)].count(i) for i in range(6)]
                where[5] += max(len(later) - 6, 0)

                def some(i):
                    for _ in range(where[i]):
                        u = later.pop(0)
                        if u == 0 and not head:
                            pe.wait_ge(mrow_ready, 2 * mp_of)
                        if u == MAX_BEFORE and not head:
                            pe.wait_ge(mrow_ready, 2 * mp_of + 1)
                        max_tile(mp_of, DOT, 1 + mpar, mp_of // 2 + 1, u)

                before = (it, kind, s - 1) if s else (it - 1, 1 - kind, NSTEP - 1)
                has_before = not (head and s == 0)
                scores(it, which, s, 0, head)
                some(0)
                scores(it, which, s, 1, head)
                some(1)
                if has_before:
                    times_v(*before, 0, head)
                some(2)
                scores(it, which, s, 2, head)
                some(3)
                scores(it, which, s, 3, head)
                some(4)
                if has_before:
                    times_v(*before, 1, head)
                some(5)
                if s == MT_STEP and not last:
                    if kind == GEO:
                        max_rows(p, DOT)
                    else:
                        pe.wait_ge(mx_free[DOT], (p + 1) * NMX + MAX_BEFORE)
                        wide_maxima(p + 1)
                for qt in range(NQT):
                    if s - 2 == LAST_OF[qt]:
                        turn(it, qt)
                if s == 1 and not head:
                    turn(it - 1, NQT - 1)

            def item(p, kind, par, head, maxima, last):
                for j in range(2):
                    if kind == GEO:
                        pe.wait_ge(qk_in[0][j], (p + 1) * 12 * 16)
                    else:
                        pe.wait_ge(qk_in[1 + par][j], (p // 2 + 1) * 12 * 16)
                pe.wait_ge(m_in, (2 * p + kind + 1) * 32)
                for s in range(NSTEP):
                    step(p, kind, par, s, head, maxima, last)

            def pair(p, par, first, last):
                item(p, GEO, par, first, MAX_IN_FIRST if first else MAX_IN_GEO, False)
                if first:
                    pe.wait_ge(ones_ready, 5)
                item(p, DOT, par, False, NO_MAXIMA if last else MAX_IN_DOT, last)

            wide_maxima(0)
            pair(0, 0, True, False)
            with pe.Fori(0, NPAIR // 2 - 1) as k:
                pair(2 * k + 1, 1, False, False)
                pair(2 * k + 2, 0, False, False)
            pair(NPAIR - 1, 1, False, True)
            for j in range(2):
                times_v(ITEMS - 1, DOT, NSTEP - 1, j, False)
            turn(ITEMS - 1, NQT - 1)

        @block.scalar
        def _(act):
            def item(it, head):
                for n in range(NEX):
                    s = n // HG
                    _, w = place(s)
                    act.wait_ge(ex_ready, it * NEX + n + 1)
                    if n % HG == 0 and not (head and s < 2):
                        act.wait_ge(pv_step, it * NSTEP + s - 1)
                    act.activation(prob[n % 8][:, 0:w], ex[:, n % 2, 0:w], ACT.Exp).then_inc(ex_done, 1)

            item(0, True)
            with act.Fori(1, ITEMS) as it:
                item(it, False)

        @block.vector
        def _(v):
            v.wait_ge(ones_ready, 3)
            is_wide = v.value_load(wide[0:1, 0:1], min_val=0, max_val=1)

            def max_tile(p, kind, u):
                h, qb, k0, w, _ = MAXT[u]
                v.wait_ge(mx_ready[kind], p * (NMX * COUNT[kind]) + (u + 1) * COUNT[kind])
                v.tensor_reduce(out=mp[kind][:, h * NKB + qb, k0 // CH:k0 // CH + 1], in_=mx[:, u % 2, 0:w],
                                axis=AX.X, op=ALU.max).then_inc(mx_free[kind], COUNT[kind])

            def rows_free(it, first):
                if not first:
                    v.wait_ge(m_in, it * 32)

            def max_rows(p, kind, first):
                v.wait_ge(mx_free[kind], p * (NMX * COUNT[kind]) + NMT * COUNT[kind])
                v.tensor_reduce(out=negm[:, 0:HG * NKB], in_=mp[kind][:, :, :], axis=AX.X, op=ALU.max,
                                negate=True).then_inc(negm_ready[kind], 1)
                v.wait_ge(mx_ready[kind], (p + 1) * (NMX * COUNT[kind]))
                rows_free(2 * p + kind, first)
                src = mx[0:HG * NKB, 0, 0:P]
                v.tensor_copy(mrow[:, 0, :], src).then_inc(mx_free[kind], COUNT[kind])
                v.wait_ge(mx_free[kind], (p + 1) * (NMX * COUNT[kind]))
                v.tensor_tensor(out=mrow[:, 1, :], in0=src, in1=mrow[:, 0, :], op=ALU.subtract)\
                 .then_inc(mrow_ready, 1)

            def geo_rows(p, first):
                with v.If(is_wide > 0):
                    for u in range(NMT):
                        max_tile(p, GEO, u)
                    max_rows(p, GEO, first)
                with v.If(is_wide == 0):
                    rows_free(2 * p, first)
                    v.memset(mrow[:, :, :], 0.0).then_inc(mrow_ready, 1)

            def take(it, qt, head):
                v.wait_ge(pv_step, it * NSTEP + LAST_OF[qt] + 1)
                if not (head and qt < 2):
                    v.wait_ge(tr_done, it * NQT + qt - 1)
                v.tensor_copy(ot[qt % 2][:, :], pv[:, qt % 2, :]).then_inc(ot_ready, 1)

            def normalise(it, qt, head):
                v.wait_ge(tr_done, it * NQT + qt + 1)
                if not (head and qt < 2):
                    v.wait_ge(on_st[qt % 2], (it * (NQT // 2) + qt // 2) * 16)
                src = pv[:, qt % 2, :].rearrange("p (n w) -> p n w", w=VW)
                v.reciprocal(rz[:, :].unsqueeze(2), src[:, :, DH:DH + 1]).then_inc(rz_ready, 1)
                v.wait_ge(rz_ready, it * NQT + qt + 1)
                v.tensor_tensor(out=on[qt % 2][:, :, :].rearrange("p s (h d) -> p (s h) d", d=DH),
                                in0=src[:, :, 0:DH], in1=rz[:, :].unsqueeze(2).to_broadcast([P, TT * HG, DH]),
                                op=ALU.mult).then_inc(on_ready, 1)

            def item(p, kind, head, maxima, last):
                it = 2 * p + kind
                for s in range(NSTEP):
                    for u in maxima[s]:
                        max_tile(p if kind == GEO else p + 1, DOT, u)
                    if s == MT_STEP and not last:
                        if kind == GEO:
                            max_rows(p, DOT, False)
                        else:
                            geo_rows(p + 1, False)
                    if s == 0 and not head:
                        take(it - 1, NQT - 1, False)
                    if s == 1 and not head:
                        normalise(it - 1, NQT - 1, False)
                    for qt in range(NQT):
                        if s - 1 == LAST_OF[qt]:
                            take(it, qt, head)
                        if s - 2 == LAST_OF[qt]:
                            normalise(it, qt, head)

            def pair(p, first, last):
                item(p, GEO, first, MAX_IN_FIRST if first else MAX_IN_GEO, False)
                item(p, DOT, False, NO_MAXIMA if last else MAX_IN_DOT, last)

            geo_rows(0, True)
            pair(0, True, False)
            with v.Fori(1, NPAIR - 1) as p:
                pair(p, False, False)
            pair(NPAIR - 1, False, True)
            take(ITEMS - 1, NQT - 1, False)
            normalise(ITEMS - 1, NQT - 1, False)


def finish(nc, x, heads, gate_z, ident, weights, out):
    NT = NC * TT
    NM = HID // P
    FIRST, SECOND = 0, 1
    with ExitStack() as ctx:
        def sb(name, shape, dt=F32):
            return ctx.enter_context(nc.sbuf_tensor(name, shape, dt))

        def pb(name, shape):
            return ctx.enter_context(nc.psum_tensor(name, shape, F32))

        def sem(name):
            return ctx.enter_context(nc.semaphore(name))

        wo, ob, wgf, wuf, wdf = (weights[n] for n in ("out", "out_b", "gate", "up", "down"))
        ez = sb("ez", [P, NT, H])
        gsum = sb("gsum", [P, NT])
        gate = sb("gate", [P, NT])
        omg = sb("omg", [P, NT])
        att = [[sb(f"att{a}_{i}", [P, TT, D]) for i in range(2)] for a in range(2)]
        xin = [sb(f"xin{i}", [P, TT, D]) for i in range(2)]
        mix = sb("mix", [P, TT, D])
        mix_t = sb("mix_t", [P, NK, CH])
        y = [sb(f"y{i}", [P, TT, D]) for i in range(2)]
        y_t = sb("y_t", [P, NK, CH])
        sums = [sb(f"sums{i}", [P, TT, D]) for i in range(2)]
        stat = sb("stat", [P, 2, TT, 6])
        mean_var = sb("mean_var", [P, 2, TT, 2])
        var_eps = sb("var_eps", [P, 2, TT])
        std = sb("std", [P, 2, TT])
        rstd = sb("rstd", [P, 2, TT])
        sg = [sb(f"sg{i}", [P, CH]) for i in range(2)]
        ht = sb("ht", [P, NM, CH])
        res = [sb(f"res{i}", [P, TT, D]) for i in range(2)]
        pt = pb("pt", [P, NK, CH])
        pg = [pb(f"pg{i}", [P, 2, CH]) for i in range(2)]
        po = [pb(f"po{i}", [P, CH]) for i in range(2)]

        att_in = [sem(f"att_in{i}") for i in range(2)]
        xin_in = [sem(f"xin_in{i}") for i in range(2)]
        e_ready = sem("e_ready")
        dve = sem("dve3")
        gate_ready = sem("gate_ready")
        xb_ready = sem("xb_ready")
        mix_tmp = sem("mix_tmp")
        mix_ready = sem("mix_ready")
        mix_turned = sem("mix_turned")
        mix_t_ready = sem("mix_t_ready")
        y_turned = sem("y_turned")
        y_t_ready = sem("y_t_ready")
        prod_ready = [sem(f"prod_ready{i}") for i in range(2)]
        sums_ready = [sem(f"sums_ready{i}") for i in range(2)]
        stat_ready = [sem(f"stat_ready{i}") for i in range(2)]
        mv_ready = [sem(f"mv_ready{i}") for i in range(2)]
        var_ready = [sem(f"var_ready{i}") for i in range(2)]
        std_ready = sem("std_ready")
        rstd_ready = sem("rstd_ready")
        normed = [sem(f"normed{i}") for i in range(2)]
        pg_ready = sem("pg_ready")
        sg_ready = sem("sg_ready")
        ht_ready = sem("ht_ready")
        res_st = [sem(f"res_st{i}") for i in range(2)]
        passed = sem("sp_passed3")
        v_passed = sem("v_passed")
        block = ctx.enter_context(nc.Block())

        x_v = x.rearrange("(c t p) n -> c p t n", p=P, t=TT)
        out_v = out.rearrange("(c t p) n -> c p t n", p=P, t=TT)
        heads_v = heads[:, :, :, :].rearrange("(b g a) p k n -> a b g p k n", a=2, b=B)


        @block.sync
        def _(q):
            def load_att(c, par):
                for a in range(2):
                    for g in range(NG):
                        q.dma_start(att[a][par][:, :, g * HG * DH:(g + 1) * HG * DH],
                                    heads_v[a, c // CPB, g, :, bass.ds((c % CPB) * TT, TT), :])\
                         .then_inc(att_in[par], 16)

            def load_x(c, par):
                q.dma_start(xin[par][:, :, :], x_v[c]).then_inc(xin_in[par], 16)

            def round_(c, par, more_x, more_att, has_second):
                if more_x:
                    q.wait_ge(sums_ready[FIRST], (c + 2) * TT)
                    q.sem_inc(passed, 1)
                    load_x(c + 3, 1 - par)
                if more_att:
                    q.wait_ge(mix_ready, (c + 3) * TT)
                    q.sem_inc(passed, 1)
                    load_att(c + 4, par)
                if has_second:
                    q.wait_ge(normed[SECOND], c * TT)
                    q.sem_inc(passed, 1)
                    q.dma_start(out_v[c - 1], res[1 - par][:, :, :]).then_inc(res_st[1 - par], 16)

            load_att(0, 0)
            load_x(0, 0)
            load_att(1, 1)
            load_x(1, 1)
            for c in range(2):
                q.wait_ge(mix_ready, (c + 1) * TT)
                load_att(c + 2, c)
            q.wait_ge(sums_ready[FIRST], TT)
            load_x(2, 0)
            round_(0, 0, True, True, False)
            with q.Fori(0, NC // 2 - 3) as k:
                round_(2 * k + 1, 1, True, True, True)
                round_(2 * k + 2, 0, True, True, True)
            for c in range(NC - 5, NC):
                round_(c, c % 2, c + 3 < NC, c + 4 < NC, True)
            q.wait_ge(normed[SECOND], NC * TT)
            q.dma_start(out_v[NC - 1], res[1][:, :, :]).then_inc(res_st[1], 16)
            for i in range(2):
                q.wait_ge(res_st[i], NC // 2 * 16)

        @block.gpsimd
        def _(g):
            with g.Fori(0, NC // 2) as k:
                for par in range(2):
                    g.wait_ge(xin_in[par], (k + 1) * 16)
                    g.tensor_tensor(out=xin[par][:, :, :], in0=xin[par][:, :, :],
                                    in1=ob[:, :].unsqueeze(1).to_broadcast([P, TT, D]), op=ALU.add)\
                     .then_inc(xb_ready, 1)

        @block.tensor
        def _(pe):
            def transposes(src):
                for k in range(NK):
                    for tt in range(TT):
                        last = pe.transpose(pt[:, k, tt * P:(tt + 1) * P], src[:, tt, k * P:(k + 1) * P],
                                            ident[:, :])
                return last

            def turn_mixed(c, head):
                pe.wait_ge(mix_ready, (c + 1) * TT)
                if not head:
                    pe.wait_ge(mix_t_ready, c)
                    if not isinstance(c, int) or c > 1:
                        pe.wait_ge(y_t_ready, c)
                transposes(mix).then_inc(mix_turned, 1)

            def turn_normed(c, par, mixed_before):
                pe.wait_ge(normed[FIRST], (c + 1) * TT)
                pe.wait_ge(mix_t_ready, mixed_before)
                transposes(y[par]).then_inc(y_turned, 1)

            def out_chunk(c, head, second):
                pe.wait_ge(mix_t_ready, c + 1)
                for tt in range(TT):
                    if tt >= 2:
                        pe.wait_ge(sums_ready[FIRST], c * TT + tt - 1)
                    elif second:
                        pe.wait_ge(sums_ready[FIRST], c * TT)
                    elif not head:
                        pe.wait_ge(sums_ready[SECOND], (c - 2) * TT + tt + 3)
                    for k in range(NK):
                        last = pe.matmul(po[tt % 2][:, 0:D], mix_t[:, k, tt * P:(tt + 1) * P], wo[:, k, :],
                                         start=k == 0, stop=k == NK - 1)
                    last.then_inc(prod_ready[FIRST], 1)

            def hidden(c, head):
                pe.wait_ge(y_t_ready, c + 1)
                for m in range(NM):
                    if not (head and m < 2):
                        pe.wait_ge(ht_ready, c * NM + m - 1)
                    for i, w in enumerate((wgf, wuf)):
                        for k in range(NK):
                            last = pe.matmul(pg[m % 2][:, i, :], w[:, k, m * P:(m + 1) * P], y_t[:, k, :],
                                             start=k == 0, stop=k == NK - 1)
                    last.then_inc(pg_ready, 1)

            def down(c, tts, has_first):
                if 0 in tts:
                    pe.wait_ge(ht_ready, (c + 1) * NM)
                for tt in tts:
                    if tt >= 2:
                        pe.wait_ge(sums_ready[SECOND], c * TT + tt - 1)
                    elif has_first:
                        pe.wait_ge(sums_ready[FIRST], (c + 1) * TT + tt + 3)
                    else:
                        pe.wait_ge(sums_ready[SECOND], (c - 1) * TT + tt + 3)
                    for m in range(NM):
                        last = pe.matmul(po[tt % 2][:, 0:D], ht[:, m, tt * P:(tt + 1) * P], wdf[:, m, :],
                                         start=m == 0, stop=m == NM - 1)
                    last.then_inc(prod_ready[SECOND], 1)

            def round_(c, par, head, has_first, has_mix):
                if has_first:
                    out_chunk(c + 1, False, head)
                hidden(c, head)
                if has_first:
                    turn_normed(c + 1, 1 - par, c + 2)
                down(c, (0, 1), has_first)
                if has_mix:
                    turn_mixed(c + 2, False)
                down(c, (2, 3), has_first)

            turn_mixed(0, True)
            out_chunk(0, True, False)
            turn_mixed(1, False)
            turn_normed(0, 0, 2)
            round_(0, 0, True, True, True)
            with pe.Fori(0, NC // 2 - 2) as k:
                round_(2 * k + 1, 1, False, True, True)
                round_(2 * k + 2, 0, False, True, True)
            round_(NC - 3, 1, False, True, True)
            round_(NC - 2, 0, False, True, False)
            round_(NC - 1, 1, False, False, False)

        @block.scalar
        def _(act):
            act.activation(ez[:, :, :], gate_z[:, :, :], ACT.Exp, scale=-1.0).then_inc(e_ready, 1)

            def mixed_columns(c, head):
                act.wait_ge(mix_turned, c + 1)
                if not head:
                    act.wait_ge(prod_ready[FIRST], c * TT)
                act.activation(mix_t[:, :, :], pt[:, :, :], ACT.Copy).then_inc(mix_t_ready, 1)

            def normed_columns(c, head):
                act.wait_ge(y_turned, c + 1)
                if not head:
                    act.wait_ge(pg_ready, c * NM)
                act.activation(y_t[:, :, :], pt[:, :, :], ACT.Copy).then_inc(y_t_ready, 1)

            def roots(first, second):
                lo, hi = (0 if first is not None else 1), (2 if second is not None else 1)
                if first is not None:
                    act.wait_ge(var_ready[FIRST], first)
                if second is not None:
                    act.wait_ge(var_ready[SECOND], second)
                act.activation(std[:, lo:hi, :], var_eps[:, lo:hi, :], ACT.Sqrt).then_inc(std_ready, 1)

            def round_(c, head, has_first, has_mix):
                for m in range(NM):
                    act.wait_ge(pg_ready, c * NM + m + 1)
                    if not (head and m < 2):
                        act.wait_ge(ht_ready, c * NM + m - 1)
                    act.activation(sg[m % 2][:, :], pg[m % 2][:, 0, :], ACT.Silu, scale=SCALE_W)\
                       .then_inc(sg_ready, 1)
                    if m == 1:
                        roots(c + 2 if has_first else None, None if head else c)
                if has_first:
                    normed_columns(c + 1, False)
                if has_mix:
                    mixed_columns(c + 2, False)

            mixed_columns(0, True)
            mixed_columns(1, False)
            roots(1, None)
            normed_columns(0, True)
            round_(0, True, True, True)
            with act.Fori(1, NC - 2) as c:
                round_(c, False, True, True)
            round_(NC - 2, False, True, False)
            round_(NC - 1, False, False, False)
            roots(None, NC)

        @block.vector
        def _(v):
            v.wait_ge(e_ready, 1)
            v.tensor_scalar(ez[:, :, :], ez[:, :, :], 1.0, None, ALU.add).then_inc(dve, 1)
            v.wait_ge(dve, 1)
            v.reciprocal(ez[:, :, :], ez[:, :, :]).then_inc(dve, 1)
            v.wait_ge(dve, 2)
            v.tensor_reduce(out=gsum[:, :], in_=ez[:, :, :], axis=AX.X, op=ALU.add).then_inc(dve, 1)
            v.wait_ge(dve, 3)
            v.tensor_scalar(gate[:, :], gsum[:, :], 1.0 / H, None, ALU.mult).then_inc(gate_ready, 1)
            v.tensor_scalar(omg[:, :], gsum[:, :], -1.0 / H, 1.0, ALU.mult, ALU.add).then_inc(gate_ready, 1)
            v.wait_ge(gate_ready, 2)

            def mixed(c, par, head):
                v.wait_ge(att_in[par], (c // 2 + 1) * 8 * 16)
                if not head:
                    v.wait_ge(mix_turned, c)
                for tt in range(TT):
                    n = c * TT + tt
                    v.tensor_scalar(mix[:, tt, :], att[DOT][par][:, tt, :], omg[:, bass.ds(n, 1)], None,
                                    ALU.mult).then_inc(mix_tmp, 1)
                v.wait_ge(mix_tmp, (c + 1) * TT)
                for tt in range(TT):
                    n = c * TT + tt
                    v.scalar_tensor_tensor(out=mix[:, tt, :], in0=att[GEO][par][:, tt, :],
                                           scalar=gate[:, bass.ds(n, 1)], in1=mix[:, tt, :],
                                           op0=ALU.mult, op1=ALU.add).then_inc(mix_ready, 1)

            def add_up(c, par, norm, head):
                if not head:
                    v.wait_ge(normed[norm], c * TT)
                for tt in range(TT):
                    v.wait_ge(prod_ready[norm], c * TT + tt + 1)
                    if norm == FIRST:
                        if tt == 0:
                            v.wait_ge(xb_ready, c + 1)
                        v.tensor_tensor(out=sums[norm][:, tt, :], in0=po[tt % 2][:, 0:D], in1=xin[par][:, tt, :],
                                        op=ALU.add).then_inc(sums_ready[norm], 1)
                    else:
                        v.scalar_tensor_tensor(out=sums[norm][:, tt, :], in0=po[tt % 2][:, 0:D], scalar=SCALE_W,
                                               in1=y[par][:, tt, :], op0=ALU.mult, op1=ALU.add)\
                         .then_inc(sums_ready[norm], 1)
                v.wait_ge(sums_ready[norm], (c + 1) * TT)
                for tt in range(TT):
                    v.bn_stats(stat[:, norm, tt, :], sums[norm][:, tt, :]).then_inc(stat_ready[norm], 1)
                v.wait_ge(stat_ready[norm], (c + 1) * TT)
                v.sem_inc(v_passed, 1)
                for tt in range(TT):
                    last = v.bn_aggr(mean_var[:, norm, tt, :], stat[:, norm, tt, :])
                last.then_inc(mv_ready[norm], 1)
                v.wait_ge(mv_ready[norm], c + 1)
                v.tensor_scalar(var_eps[:, norm, :], mean_var[:, norm, :, 1], EPS, None, ALU.add)\
                 .then_inc(var_ready[norm], 1)

            def scales(n, lo, hi):
                v.wait_ge(std_ready, n)
                v.reciprocal(rstd[:, lo:hi, :], std[:, lo:hi, :]).then_inc(rstd_ready, 1)
                v.wait_ge(rstd_ready, n)

            def normalise(c, par, norm, head):
                if not head:
                    if norm == FIRST:
                        v.wait_ge(y_turned, c - 1)
                    else:
                        v.wait_ge(res_st[par], (c // 2) * 16)
                for tt in range(TT):
                    v.tensor_scalar((y, res)[norm][par][:, tt, :], sums[norm][:, tt, :],
                                    mean_var[:, norm, tt, 0:1], rstd[:, norm, tt:tt + 1],
                                    ALU.subtract, ALU.mult).then_inc(normed[norm], 1)

            def round_(c, par, has_first, has_mix, has_second, second_head):
                if has_first:
                    add_up(c + 1, 1 - par, FIRST, False)
                for m in range(NM):
                    v.wait_ge(sg_ready, c * NM + m + 1)
                    v.scalar_tensor_tensor(out=ht[:, m, :], in0=pg[m % 2][:, 1, :], scalar=SCALE_W,
                                           in1=sg[m % 2][:, :], op0=ALU.mult, op1=ALU.mult).then_inc(ht_ready, 1)
                    if m == 1:
                        scales(c + 2, 0 if has_first else 1, 2 if has_second else 1)
                        if has_first:
                            normalise(c + 1, 1 - par, FIRST, isinstance(c, int) and c == 0)
                    if m == 2 and has_mix:
                        mixed(c + 2, par, False)
                    if m == 3 and has_second:
                        normalise(c - 1, 1 - par, SECOND, second_head)
                add_up(c, par, SECOND, not has_second)

            mixed(0, 0, True)
            mixed(1, 1, False)
            add_up(0, 0, FIRST, True)
            scales(1, 0, 1)
            normalise(0, 0, FIRST, True)
            round_(0, 0, True, True, False, True)
            for c in (1, 2):
                round_(c, c % 2, True, True, True, True)
            with v.Fori(1, NC // 2 - 2) as k:
                round_(2 * k + 1, 1, True, True, True, False)
                round_(2 * k + 2, 0, True, True, True, False)
            round_(NC - 3, 1, True, True, True, False)
            round_(NC - 2, 0, True, False, True, False)
            round_(NC - 1, 1, False, False, True, False)
            scales(NC + 2, 1, 2)
            normalise(NC - 1, 1, SECOND, False)


_INPUTS = ("xt", "x", "w_qk", "b_qk", "w_v", "w_line", "b_v", "b_gate", "inc", "out_w", "out_b", "wg", "wu", "wd")


def kernel(**inputs):
    import numpy as np
    import concourse.bacc as bacc
    from concourse.bass_utils import run_bass_kernel_spmd as run

    a = {k[3:]: np.asarray(v) for k, v in inputs.items()}
    x = a["attn_x"].reshape(B * T, D)
    padded = np.zeros((B, D, T + 1), x.dtype)
    padded[:, :, 1:] = x.reshape(B, T, D).transpose(0, 2, 1)
    xt = np.stack([padded[c // CPB, :, (c % CPB) * CH:(c % CPB) * CH + CH + 1] for c in range(NC)])
    qkv_w, qkv_b = a["attn_qkv_w"], a["attn_qkv_b"]
    laid = {
        "xt": xt, "x": x,
        "w_qk": qkv_w[:, :2 * D], "b_qk": qkv_b[:2 * D].reshape(4, P).T,
        "w_v": np.concatenate([qkv_w[:, 2 * D:], a["attn_geo_w"]], 1),
        "w_line": np.concatenate([a["attn_w1_write"], a["attn_w2_write"], a["attn_w1_read"],
                                  a["attn_w2_read"], a["attn_gate_w"]], 1),
        "b_v": np.concatenate([qkv_b[2 * D:], a["attn_geo_b"]]), "b_gate": a["attn_gate_b"],
        "inc": a["attn_inc_scale"], "out_w": a["attn_out_w"], "out_b": a["attn_out_b"],
        "wg": a["ffn_w_gate"].T, "wu": a["ffn_w_up"].T, "wd": a["ffn_w_down"].T,
    }
    nc = bacc.Bacc("TRN2", target_bir_lowering=False, num_devices=1)
    arrays, args = {}, []
    for name in _INPUTS:
        arr = np.ascontiguousarray(laid[name])
        arrays[f"in_{name}"] = arr
        args.append(nc.dram_tensor(f"in_{name}", arr.shape, mybir.dt.from_np(arr.dtype), kind="ExternalInput").ap())
    out = nc.dram_tensor("out_0", (B * T, D), F32, kind="ExternalOutput").ap()
    build(nc, *args, out)
    r = run(nc, [arrays], core_ids=[0])
    return r.results[0]["out_0"].reshape(B, T, D)
```
